# Optimizing a Trainium2 kernel written in Bass

```python
import numpy as np
import jax
import jax.numpy as jnp

def _softmax(x, axis=-1):
    return jax.nn.softmax(x, axis=axis)

def _gelu(x):
    return jax.nn.gelu(x, approximate=True)

def _silu(x):
    return jax.nn.silu(x)

def _sigmoid(x):
    return jax.nn.sigmoid(x)

def _layernorm(x, axis=-1, eps=1e-05):
    m = jnp.mean(x, axis=axis, keepdims=True)
    v = jnp.var(x, axis=axis, keepdims=True)
    return (x - m) / jnp.sqrt(v + eps)

def _scatter_add(tgt, idx, src, axis=0):
    return tgt.at[idx].add(src)

def _segment_sum(src, seg, n):
    return jax.ops.segment_sum(src, seg, n)
kernel_name = 'mk_seq_preln_d1_jaxref_r8_a2981b'

def setup_inputs(seed: int=0):
    np.random.seed(seed)
    _w = jnp.asarray

    def _L0_attn_setup():
        import jax, jax.numpy as jnp
        import numpy as np
        D_K, D_MODEL, NUM_HEADS = (64, 128, 16)

        def _xavier(key, shape):
            fan_in, fan_out = (shape[-2], shape[-1])
            limit = float(np.sqrt(6.0 / (fan_in + fan_out)))
            return jax.random.uniform(key, shape, jnp.float32, -limit, limit)
        key = jax.random.key(seed)
        kx, kq, kk, kv, ko = jax.random.split(key, 5)
        x = jax.random.normal(kx, (2, 256, D_MODEL), dtype=jnp.float32)
        w_q = _xavier(kq, (NUM_HEADS, D_MODEL, D_K))
        w_k = _xavier(kk, (NUM_HEADS, D_MODEL, D_K))
        w_v = _xavier(kv, (NUM_HEADS, D_MODEL, D_K))
        w_o = _xavier(ko, (NUM_HEADS * D_K, D_MODEL))
        return {'x': x, 'w_q': w_q, 'w_k': w_k, 'w_v': w_v, 'w_o': w_o}
    _L0_attn_in = _L0_attn_setup()

    def _L0_ffn_setup():
        import math
        import jax, jax.numpy as jnp
        import numpy as np
        B, S, D, F, E = (8, 256, 128, 512, 8)
        CAPACITY_FACTOR = 1.0
        key = jax.random.key(seed)
        k1, k2, k3, k4 = jax.random.split(key, 4)
        x = jax.random.normal(k1, (B, S, D), dtype=jnp.float32)
        Wr = jax.random.normal(k2, (D, E), dtype=jnp.float32) * (1.0 / math.sqrt(D))
        W1 = jax.random.normal(k3, (E, D, F), dtype=jnp.float32) * (1.0 / math.sqrt(D))
        W2 = jax.random.normal(k4, (E, F, D), dtype=jnp.float32) * (1.0 / math.sqrt(F))
        return {'x': x, 'Wr': Wr, 'W1': W1, 'W2': W2}
    _L0_ffn_in = _L0_ffn_setup()
    _d = {'L0_attn_x': _L0_attn_in['x'], 'L0_attn_w_q': _L0_attn_in['w_q'], 'L0_attn_w_k': _L0_attn_in['w_k'], 'L0_attn_w_v': _L0_attn_in['w_v'], 'L0_attn_w_o': _L0_attn_in['w_o'], 'L0_ffn_Wr': _L0_ffn_in['Wr'], 'L0_ffn_W1': _L0_ffn_in['W1'], 'L0_ffn_W2': _L0_ffn_in['W2']}
    _x0 = _d['L0_attn_x']
    _d['L0_attn_x'] = jax.random.normal(jax.random.fold_in(jax.random.key(seed), 1), (4, 1024, 128), dtype=_x0.dtype)
    del _x0
    return _d

def reference(L0_attn_x, L0_attn_w_q, L0_attn_w_k, L0_attn_w_v, L0_attn_w_o, L0_ffn_Wr, L0_ffn_W1, L0_ffn_W2):

    def _L0_attn_ref(x, w_q, w_k, w_v, w_o):
        import jax, jax.numpy as jnp
        import numpy as np
        D_K, D_MODEL, NUM_HEADS = (64, 128, 16)

        def _xavier(key, shape):
            fan_in, fan_out = (shape[-2], shape[-1])
            limit = float(np.sqrt(6.0 / (fan_in + fan_out)))
            return jax.random.uniform(key, shape, jnp.float32, -limit, limit)
        scale = 1.0 / jnp.sqrt(jnp.asarray(D_K, dtype=jnp.float32))
        q = jnp.einsum('bsd,hdk->bhsk', x, w_q)
        k = jnp.einsum('bsd,hdk->bhsk', x, w_k)
        v = jnp.einsum('bsd,hdk->bhsk', x, w_v)
        scores = jnp.einsum('bhqk,bhmk->bhqm', q, k) * scale
        weights = jax.nn.softmax(scores, axis=-1)
        z = jnp.einsum('bhqm,bhmk->bhqk', weights, v)
        b, h, s, dk = z.shape
        z = jnp.transpose(z, (0, 2, 1, 3)).reshape(b, s, h * dk)
        z = jnp.einsum('bse,ed->bsd', z, w_o)
        return x + z

    def _L0_ffn_ref(x, Wr, W1, W2):
        import math
        import jax, jax.numpy as jnp
        import numpy as np
        B, S, D, F, E = (8, 256, 128, 512, 8)
        CAPACITY_FACTOR = 1.0
        b, s, d = x.shape
        t = b * s
        cap = max(math.ceil(t * CAPACITY_FACTOR / E), 1)
        xf = x.reshape(t, d)
        probs = jax.nn.softmax(xf.astype(jnp.float32) @ Wr, axis=-1)
        eidx = jnp.argmax(probs, axis=-1)
        p_tok = jnp.take_along_axis(probs, eidx[:, None], axis=1)[:, 0]
        onehot = jax.nn.one_hot(eidx, E, dtype=jnp.int32)
        rank_all = jnp.cumsum(onehot, axis=0) - onehot
        rank = jnp.take_along_axis(rank_all, eidx[:, None], axis=1)[:, 0]
        keep = rank < cap
        slot = jnp.where(keep, rank, cap)
        dispatch = jnp.zeros((E, cap + 1), dtype=jnp.int32).at[eidx, slot].set(jnp.arange(t, dtype=jnp.int32))
        valid = jnp.zeros((E, cap + 1), dtype=bool).at[eidx, slot].set(keep)
        dispatch = dispatch[:, :cap]
        valid = valid[:, :cap]
        xe = xf[dispatch]
        h = jnp.maximum(jnp.einsum('ecd,edf->ecf', xe, W1), 0.0)
        ye = jnp.einsum('ecf,efd->ecd', h, W2)
        pe = p_tok[dispatch]
        ye = ye * (pe * valid.astype(ye.dtype))[:, :, None]
        y = jnp.zeros((t, d), dtype=x.dtype).at[dispatch.reshape(-1)].add(ye.reshape(E * cap, d).astype(x.dtype))
        return y.reshape(b, s, d)
    x = L0_attn_x
    x = x + _L0_attn_ref(_layernorm(x, axis=-1), L0_attn_w_q, L0_attn_w_k, L0_attn_w_v, L0_attn_w_o)
    x = x + _L0_ffn_ref(_layernorm(x, axis=-1), L0_ffn_Wr, L0_ffn_W1, L0_ffn_W2)
    return x

_drawn_inputs = setup_inputs


def setup_inputs(seed=0):
    import zlib

    import numpy as np

    out = dict(_drawn_inputs(seed))
    spreads = {}
    factors = {}
    for name, (base, spread) in spreads.items():
        noise = np.random.default_rng([zlib.crc32(name.encode()), seed]).standard_normal(out[name].shape)
        drawn = base * np.exp(spread * noise) if base else spread * noise
        out[name] = jnp.asarray(drawn.astype(out[name].dtype))
    for name, factor in factors.items():
        out[name] = (out[name] * factor).astype(out[name].dtype)
    return out
```

```python
from contextlib import ExitStack

import concourse.bass as bass
from concourse import mybir

F32 = mybir.dt.float32
F32R = mybir.dt.float32r
I32 = mybir.dt.int32
U32 = mybir.dt.uint32
BF16 = mybir.dt.bfloat16
ALU = mybir.AluOpType
ACT = mybir.ActivationFunctionType
AX_X = mybir.AxisListType.X

P = 128
HALF = 512
EPS = 1e-5

QK_AT = {0: 0, 1: 1, 4: 2, 6: 3}
V_AT = {8: 0, 9: 1}
C_AT = {17: 0, 25: 1}
SUM_AT = {24: 0, 28: 1}
RECIP_AT = {25: (0, 0), 26: (0, 1), 27: (0, 2), 28: (0, 3), 29: (1, 0), 30: (1, 1), 31: (1, 2), 32: (1, 3)}
WO_AT = {14: 0, 19: 1}
MAX_FROM, MAX_TO = 4, 25
UNITS = 32
LOW_Q, LOW_K = 1, 2
Z_AT = {3: 0, 4: 1}


def max_units(u):
    def before(v):
        return UNITS * min(max(v - MAX_FROM, 0), MAX_TO - MAX_FROM) // (MAX_TO - MAX_FROM)
    return range(before(u), before(u + 1))


def block_kernel(nc, x_in, w_q, w_k, w_v, w_o, w_r, w_1, w_2, out):
    B, S, D = x_in.shape
    H, _, DK = w_q.shape
    E, _, F = w_1.shape
    T = B * S
    TT = T // P
    QT = S // P
    KT = S // P
    PAIRS = B * H // 2
    HP = H // 2
    CAP = -(-T // E)
    FC = F // P
    ST = CAP // P
    SCALE = 1.0 / float(DK) ** 0.5
    NB = 8
    KB = DK + NB
    RING = 4
    assert D == P and 2 * DK == P and 2 * HALF == S and QT == NB and CAP == HALF and PAIRS % 2 == 0
    assert UNITS == 4 * KT

    x_t = x_in.rearrange("b (n p) d -> b p n d", p=P)
    out_t = out.rearrange("b (n p) d -> b p n d", p=P)
    wq_d = w_q.rearrange("h d k -> d h k")
    wk_d = w_k.rearrange("h d k -> d h k")
    wv_d = w_v.rearrange("h d k -> d h k")
    wo_d = w_o.rearrange("(h p) d -> p h d", p=P)
    slots_d = nc.dram_tensor("tokens_by_slot", (E * CAP + T, D), F32, kind="Internal").ap()
    made_d = nc.dram_tensor("outputs_by_slot", (E * CAP, D), F32, kind="Internal").ap()

    with ExitStack() as ctx:
        def sb(name, shape, dt=F32):
            return ctx.enter_context(nc.sbuf_tensor(name, shape, dt))

        def sem(name):
            return ctx.enter_context(nc.semaphore(name))

        x2 = sb("x2", [P, TT * D])
        ring = sb("ring", [P, RING * 2 * S])
        ident = sb("ident", [P, P])
        upper = sb("upper", [P, P], BF16)
        ones_b = sb("ones_b", [P, P], BF16)
        zeros = sb("zeros", [P, S])
        stats = sb("stats", [P, 8 * QT])
        wr = sb("wr", [P, E])
        lg, ex, hot, cand, iota_e = (sb(n, [P, TT * E])[:, :].rearrange("p (t e) -> p t e", e=E)
                                     for n in ("logits", "shifted_logits", "one_hot", "candidate", "expert_no"))
        hot_b = sb("one_hot_b", [P, TT * E], BF16)
        cols = sb("routing_columns", [P, 11, TT])
        token_no = sb("token_no", [P, TT])
        scatter_at = sb("scatter_at", [P, TT], I32)
        gather_at = sb("gather_at", [P, TT], I32)

        with ExitStack() as later:
            def sb_later(name, shape):
                return later.enter_context(nc.sbuf_tensor(name, shape, F32))

            w1_sb = sb_later("w1", [P, E * F])
            w2_sb = sb_later("w2", [P, FC * E * D])
            xe = [sb_later(f"xe{i}", [P, HALF]) for i in range(2)]
            xeT = [sb_later(f"xeT{i}", [P, HALF]) for i in range(2)]
            rT = [sb_later(f"rT{i}", [P, FC * HALF]) for i in range(2)]
            ye = [sb_later(f"ye{i}", [P, HALF]) for i in range(2)]

        kA = [[sb(f"kA{i}{p}", [P, S], F32R) for p in range(2)] for i in range(2)]
        qA = [[sb(f"qA{i}{p}", [P, S], F32R) for p in range(2)] for i in range(2)]
        kB = [[sb(f"kB{i}{p}", [KB, S], F32R) for p in range(2)] for i in range(2)]
        qB = [[sb(f"qB{i}{p}", [KB, S], F32R) for p in range(2)] for i in range(2)]
        hT = sb("hT", [P, T])
        hTs = [sb(f"hTs{i}", [P, S]) for i in range(2)]
        wst = [sb(f"wst{i}", [P, 6 * DK]) for i in range(2)]
        wo = [sb(f"wo{i}", [P, D]) for i in range(2)]
        V = [sb(f"V{i}", [P, KT * P]) for i in range(2)]
        acc = [sb(f"acc{i}", [P, 2 * S]) for i in range(2)]
        zr = sb("zr", [P, S])
        zT = sb("zT", [P, S])
        rc = sb("rc", [P, S])
        mxp = [sb(f"mxp{p}", [P, QT, 2]) for p in range(2)]
        mxw = [sb(f"mxw{p}", [P, KB]) for p in range(2)]
        rowmask = sb("rowmask", [KB, S])
        ones = sb("ones", [P, DK])

        def P_tile(kt, p, half):
            at = ((kt % RING) * 2 + p) * S + half * HALF
            return ring[:, at:at + HALF]

        ps_s = [ctx.enter_context(nc.psum_tensor(f"ps_s{i}", [P, HALF], F32)) for i in range(2)]
        ps_m = [ctx.enter_context(nc.psum_tensor(f"ps_m{i}", [P, HALF], F32)) for i in range(2)]
        ps_z = [ctx.enter_context(nc.psum_tensor(f"ps_z{i}", [P, HALF], F32)) for i in range(2)]
        ps_x = [ctx.enter_context(nc.psum_tensor(f"ps_x{i}", [P, HALF], F32)) for i in range(2)]

        x_loaded = [sem(f"x_loaded{b}") for b in range(B)]
        w_loaded = [sem(f"w_loaded{i}") for i in range(2)]
        wo_loaded = [sem(f"wo_loaded{i}") for i in range(2)]
        wr_loaded = sem("wr_loaded")
        consts = sem("consts")
        dve_consts = sem("dve_consts")
        chain = sem("chain")
        centred = sem("centred")
        squared = sem("squared")
        var_ready = sem("var_ready")
        root_ready = sem("root_ready")
        h_ready = sem("h_ready")
        residual_ready = sem("residual_ready")
        h_turned = sem("h_turned")
        hT_ready = sem("hT_ready")

        qk_done = sem("qk_done")
        qk_cast = sem("qk_cast")
        qk_cast_again = sem("qk_cast_again")
        qk_low = sem("qk_low")
        v_done = sem("v_done")
        v_copied = sem("v_copied")
        m_done = sem("m_done")
        maxed = sem("maxed")
        mx_ready = sem("mx_ready")
        c_done = sem("c_done")
        c_placed = sem("c_placed")
        scores_ready = sem("scores_ready")
        exp_done = sem("exp_done")
        pv_done = sem("pv_done")
        summed = sem("summed")
        sums_done = sem("sums_done")
        z_copied = sem("z_copied")
        recip_done = sem("recip_done")
        z_ready = sem("z_ready")
        wo_done = sem("wo_done")
        wo_added = sem("wo_added")

        zeroed = sem("zeroed")
        w1_loaded = sem("w1_loaded")
        w2_loaded = sem("w2_loaded")
        h2T_ready = sem("h2T_ready")
        h2_turned = sem("h2_turned")
        logits_done = sem("logits_done")
        shifted = sem("shifted")
        route_exp = sem("route_exp")
        onehot_ready = sem("onehot_ready")
        ranks_done = sem("ranks_done")
        index_ready = sem("index_ready")
        scattered = sem("scattered")
        xe_loaded = [sem(f"xe_loaded{i}") for i in range(2)]
        xe_turned = sem("xe_turned")
        xeT_ready = sem("xeT_ready")
        up_done = sem("up_done")
        relu_done = sem("relu_done")
        down_done = sem("down_done")
        ye_copied = sem("ye_copied")
        ye_stored = [sem(f"ye_stored{i}") for i in range(2)]
        gathered = sem("gathered")
        out_ready = sem("out_ready")
        stored = sem("stored")

        def h_tok(b):
            return ring[:, b * S:(b + 1) * S]

        h2T = ring[:, T:2 * T]
        square = ring[:, T:T + S]

        yg = ring[:, T:2 * T]

        block = ctx.enter_context(nc.Block())

        PAIR_LOOP = (PAIRS - 4) // 2

        @block.sync
        def _(sp):
            for b in range(B):
                sp.dma_start(x2[:, b * S:(b + 1) * S].rearrange("p (n d) -> p n d", d=D),
                             x_t[b]).then_inc(x_loaded[b], 16)
            sp.dma_start(wr[:, :], w_r).then_inc(wr_loaded, 16)

            def load_weights(j, par):
                hp, b = j % HP, j // HP
                view = wst[par][:, 0:4 * DK].rearrange("p (h t k) -> p h t k", h=2, t=2)
                sp.wait_ge(hT_ready, 2 * b + 2)
                sp.dma_start(view[:, :, 0, :], wq_d[:, bass.ds(2 * hp, 2), :]).then_inc(w_loaded[par], 16)
                sp.dma_start(view[:, :, 1, :], wk_d[:, bass.ds(2 * hp, 2), :]).then_inc(w_loaded[par], 16)
                sp.dma_start(wst[par][:, 4 * DK:6 * DK].rearrange("p (h k) -> p h k", h=2),
                             wv_d[:, bass.ds(2 * hp, 2), :]).then_inc(w_loaded[par], 16)
                sp.dma_start(hTs[par][:, :], hT[:, bass.ds(b * S, S)]).then_inc(w_loaded[par], 16)

            def load_wo(j, par):
                sp.dma_start(wo[par][:, :].rearrange("p (o d) -> p o d", o=1),
                             wo_d[:, bass.ds(j % HP, 1), :]).then_inc(wo_loaded[par], 16)

            for j in range(2):
                load_weights(j, j)
                load_wo(j, j)
            sp.wait_ge(dve_consts, 4)
            for n in range(E * CAP // S):
                sp.dma_start(slots_d[n * S:(n + 1) * S, :].rearrange("(p n) d -> p (n d)", p=P),
                             zeros[:, :]).then_inc(zeroed, 16)

            def loads(j, par):
                sp.wait_ge(v_done, 2 * j - 2)
                load_weights(j, par)
                sp.wait_ge(wo_done, 2 * j - 4)
                load_wo(j - 1, 1 - par)

            sp.wait_ge(v_done, 2)
            load_weights(2, 0)
            with sp.Fori(0, PAIR_LOOP) as i:
                for q in range(2):
                    loads(2 * i + 3 + q, (1 + q) % 2)
            loads(PAIRS - 1, (PAIRS - 1) % 2)
            sp.wait_ge(wo_done, 2 * PAIRS - 4)
            load_wo(PAIRS - 1, (PAIRS - 1) % 2)

            sp.wait_ge(scores_ready, UNITS * PAIRS)
            sp.dma_start(w1_sb[:, :].rearrange("p (e f) -> p e f", e=E),
                         w_1.rearrange("e d f -> d e f")).then_inc(w1_loaded, 16)
            for c in range(FC):
                sp.dma_start(w2_sb[:, c * E * D:(c + 1) * E * D].rearrange("p (e d) -> p e d", e=E),
                             w_2.rearrange("e (c p) d -> c p e d", p=P)[c]).then_inc(w2_loaded, 16)

            def store_made(e):
                sp.wait_ge(ye_copied, e + 1)
                sp.dma_start(made_d[e * CAP:(e + 1) * CAP, :].rearrange("(n p) d -> p n d", p=P),
                             ye[e % 2][:, :].rearrange("p (n d) -> p n d", d=D)).then_inc(ye_stored[e % 2], 16)

            sp.wait_ge(scattered, 16 * TT)
            for e in range(E):
                if e >= 2:
                    sp.wait_ge(xe_turned, e - 1)
                sp.dma_start(xe[e % 2][:, :].rearrange("p (n d) -> p n d", d=D),
                             slots_d[e * CAP:(e + 1) * CAP, :].rearrange("(n p) d -> p n d", p=P)
                             ).then_inc(xe_loaded[e % 2], 16)
                if e >= 2:
                    store_made(e - 2)
            store_made(E - 2)
            store_made(E - 1)
            for b in range(B):
                sp.wait_ge(out_ready, QT * (b + 1))
                sp.dma_start(out_t[b], x2[:, b * S:(b + 1) * S].rearrange("p (n d) -> p n d", d=D)
                             ).then_inc(stored, 16)
            sp.wait_ge(stored, 16 * B)

        @block.gpsimd
        def _(pool):
            pool.wait_ge(dve_consts, 3)
            pool.affine_select(out=ident[:, :], in_=ident[:, :], compare_op=ALU.is_equal, fill=0.0,
                               base=0, pattern=[[-1, P]], channel_multiplier=1).then_inc(consts, 1)
            pool.affine_select(out=rowmask[:, :].rearrange("p (t q) -> p t q", q=P),
                               in_=rowmask[:, :].rearrange("p (t q) -> p t q", q=P),
                               compare_op=ALU.is_equal, fill=0.0, base=-DK,
                               pattern=[[-1, NB], [0, P]], channel_multiplier=1).then_inc(consts, 1)
            pool.affine_select(out=upper[:, :], in_=upper[:, :], compare_op=ALU.is_gt, fill=0.0,
                               base=0, pattern=[[1, P]], channel_multiplier=-1).then_inc(consts, 1)
            pool.iota(token_no[:, :], pattern=[[P, TT]], base=0, channel_multiplier=1,
                      allow_small_or_imprecise_dtypes=True).then_inc(consts, 1)

            pool.iota(iota_e, pattern=[[0, TT], [1, E]], base=0, channel_multiplier=0,
                      allow_small_or_imprecise_dtypes=True).then_inc(consts, 1)

            for b in range(B):
                pool.wait_ge(h_ready, b + 1)
                pool.tensor_tensor(x2[:, b * S:(b + 1) * S], x2[:, b * S:(b + 1) * S], h_tok(b),
                                   ALU.add).then_inc(residual_ready, 1)

            def add_up(j, par):
                for kt in range(1, KT):
                    for p in range(2):
                        a = acc[par][:, p * S:(p + 1) * S]
                        n = 2 * (kt - 1) + p
                        pool.wait_ge(exp_done, UNITS * j + 4 * kt + 3 + p)
                        if kt > 1:
                            pool.wait_ge(summed, 14 * j + n - 1)
                        before = a if kt > 1 else ring[:, p * S:(p + 1) * S]
                        now = ring[:, ((kt % RING) * 2 + p) * S:((kt % RING) * 2 + p + 1) * S]
                        pool.tensor_tensor(a, before, now, ALU.add).then_inc(summed, 1)

            with pool.Fori(0, PAIRS // 2) as i:
                for par in range(2):
                    add_up(2 * i + par, par)

            pool.wait_ge(index_ready, 1)
            pool.wait_ge(zeroed, 16 * (E * CAP // S))
            for t in range(TT):
                pool.indirect_dma_start(
                    out=slots_d, out_offset=bass.IndirectOffsetOnAxis(ap=scatter_at[:, t:t + 1].bitcast(U32), axis=0),
                    in_=ring[:, t * D:(t + 1) * D], in_offset=None,
                ).then_inc(scattered, 16)
            for n in range(2):
                pool.wait_ge(ye_stored[n], 16 * (E // 2))
            pool.wait_ge(logits_done, 1)
            for t in range(TT):
                pool.indirect_dma_start(
                    out=yg[:, t * D:(t + 1) * D], out_offset=None, in_=made_d,
                    in_offset=bass.IndirectOffsetOnAxis(ap=gather_at[:, t:t + 1].bitcast(U32), axis=0),
                ).then_inc(gathered, 16)

        @block.scalar
        def _(act):
            def squares_and_root(n):
                act.wait_ge(centred, n + 1)
                act.activation(square, h_tok(n % B), ACT.Square).then_inc(squared, 1)
                act.wait_ge(var_ready, n + 1)
                act.activation(stats[:, 3 * QT:4 * QT], stats[:, 2 * QT:3 * QT], ACT.Sqrt).then_inc(root_ready, 1)

            def copy_turned(n, into, done, turned):
                act.wait_ge(turned, n + 1)
                act.activation(into[:, n * HALF:(n + 1) * HALF], ps_x[n % 2][:, :], ACT.Copy).then_inc(done, 1)

            for b in range(B):
                squares_and_root(b)
                copy_turned(2 * b, hT, hT_ready, h_turned)
                copy_turned(2 * b + 1, hT, hT_ready, h_turned)

            def cast_qk(j, par, use, again):
                p, half = divmod(use, 2)
                c = slice(half * HALF, (half + 1) * HALF)
                b = ps_x[use % 2]
                if not again:
                    act.wait_ge(qk_done, 4 * j + use + 1)
                    act.activation(qA[par][p][0:DK, c], b[0:DK, :], ACT.Copy)
                    act.activation(kA[par][p][DK:P, c], b[DK:P, :], ACT.Copy).then_inc(qk_cast, 1)
                else:
                    act.wait_ge(qk_cast, 4 * j + use + 1)
                    act.activation(qA[par][p][DK:P, c], qA[par][p][0:DK, c], ACT.Copy)
                    act.activation(kB[par][p][0:DK, c], kA[par][p][DK:P, c], ACT.Copy).then_inc(qk_cast_again, 1)

            def copy_v(j, par, half):
                act.wait_ge(v_done, 2 * j + half + 1)
                act.activation(V[par][:, half * HALF:(half + 1) * HALF], ps_x[half][:, :],
                               ACT.Copy).then_inc(v_copied, 1)

            def copy_z(j, half, first=False):
                act.wait_ge(pv_done, 2 * KT * (j + 1) - 1 + half)
                if not first:
                    act.wait_ge(z_ready, 2 * j - 1 + half)
                act.activation(zr[:, half * HALF:(half + 1) * HALF], ps_z[half][:, :], ACT.Copy).then_inc(z_copied, 1)

            def unit(j, u, first):
                kt, half, p = u // 4, (u // 2) % 2, u % 2
                if not (first and kt < RING):
                    was = kt - RING if kt >= RING else kt - RING + KT
                    back = j if kt >= RING else j - 1
                    if p == 0:
                        act.wait_ge(pv_done, 2 * KT * back + 2 * was + half + 1)
                    if half == 0:
                        act.wait_ge(summed, 14 * back + 2 * (max(was, 1) - 1) + p + 1)
                act.wait_ge(scores_ready, UNITS * j + u + 1)
                act.activation(P_tile(kt, p, half), ps_s[u % 2][:, :], ACT.Exp, scale=SCALE).then_inc(exp_done, 1)

            def pair(j, par, first=False, second=False, last=False):
                for u in range(UNITS):
                    unit(j, u, first)
                    for again in range(2):
                        if not last and u - again in QK_AT:
                            cast_qk(j + 1, 1 - par, QK_AT[u - again], again)
                    if not last and u in V_AT:
                        copy_v(j + 1, 1 - par, V_AT[u])
                    if not first and u in Z_AT:
                        copy_z(j - 1, Z_AT[u], first=second)

            for use in range(4):
                cast_qk(0, 0, use, False)
                cast_qk(0, 0, use, True)
            for half in range(2):
                copy_v(0, 0, half)
            act.wait_ge(residual_ready, B)
            pair(0, 0, first=True)
            pair(1, 1, second=True)
            with act.Fori(0, PAIR_LOOP) as i:
                for par in range(2):
                    pair(2 * i + 2 + par, par)
            pair(PAIRS - 2, 0)
            pair(PAIRS - 1, (PAIRS - 1) % 2, last=True)
            for half in range(2):
                copy_z(PAIRS - 1, half)

            for b in range(B):
                squares_and_root(B + b)
            for n in range(2 * B):
                copy_turned(n, h2T, h2T_ready, h2_turned)
            act.wait_ge(shifted, 1)
            act.activation(ex, ex, ACT.Exp).then_inc(route_exp, 1)

            def copy_made(e):
                act.wait_ge(down_done, e + 1)
                if e >= 2:
                    act.wait_ge(ye_stored[e % 2], 16 * (e // 2))
                act.activation(ye[e % 2][:, :], ps_z[e % 2][:, :], ACT.Copy).then_inc(ye_copied, 1)

            for e in range(E):
                act.wait_ge(xe_turned, e + 1)
                if e >= 2:
                    act.wait_ge(up_done, FC * (e - 1))
                act.activation(xeT[e % 2][:, :], ps_x[e % 2][:, :], ACT.Copy).then_inc(xeT_ready, 1)
                if e >= 1:
                    copy_made(e - 1)
            copy_made(E - 1)

        @block.vector
        def _(dve):
            dve.memset(ident[:, :], 1.0).then_inc(dve_consts, 1)
            dve.memset(rowmask[:, :], 1.0).then_inc(dve_consts, 1)
            dve.memset(upper[:, :], 1.0).then_inc(dve_consts, 1)
            dve.memset(zeros[:, :], 0.0).then_inc(dve_consts, 1)
            dve.memset(ones[:, :], 1.0).then_inc(dve_consts, 1)
            dve.memset(ones_b[:, :], 1.0).then_inc(dve_consts, 1)
            for p in range(2):
                dve.memset(mxw[p][:, :], 0.0).then_inc(dve_consts, 1)
                for i in range(2):
                    dve.memset(kB[i][p][DK:KB, :].bitcast(F32), -1.0).then_inc(dve_consts, 1)
            steps = [0]

            def then(ins):
                steps[0] += 1
                ins.then_inc(chain, 1)
                dve.wait_ge(chain, steps[0])

            def stat(k):
                return stats[:, k * QT:(k + 1) * QT]

            def norm(n, b):
                x3 = x2[:, b * S:(b + 1) * S].rearrange("p (t d) -> p t d", d=D)
                h3 = h_tok(b).rearrange("p (t d) -> p t d", d=D)

                def wide(a):
                    return a.rearrange("p (t o) -> p t o", o=1).to_broadcast([P, QT, D])

                then(dve.tensor_reduce(stat(0), x3, AX_X, ALU.add))
                then(dve.tensor_scalar(stat(1), stat(0), 1.0 / D, None, ALU.mult))
                dve.tensor_tensor(h3, x3, wide(stat(1)), ALU.subtract).then_inc(centred, 1)
                dve.wait_ge(squared, n + 1)
                then(dve.tensor_reduce(stat(0), square.rearrange("p (t d) -> p t d", d=D), AX_X, ALU.add))
                dve.tensor_scalar(stat(2), stat(0), 1.0 / D, EPS, ALU.mult, ALU.add).then_inc(var_ready, 1)
                dve.wait_ge(root_ready, n + 1)
                then(dve.reciprocal(stat(4), stat(3)))
                then(dve.tensor_tensor(stat(5), stat(4), stat(4), ALU.mult))
                then(dve.tensor_tensor(stat(6), stat(5), stat(2), ALU.mult))
                then(dve.tensor_scalar(stat(5), stat(6), -0.5, 1.5, ALU.mult, ALU.add))
                then(dve.tensor_tensor(stat(7), stat(5), stat(4), ALU.mult))
                dve.tensor_tensor(h3, h3, wide(stat(7)), ALU.mult).then_inc(h_ready, 1)

            for b in range(B):
                dve.wait_ge(x_loaded[b], 16)
                norm(b, b)

            def low_qk(j, par, use, of_q):
                p, half = divmod(use, 2)
                c = slice(half * HALF, (half + 1) * HALF)
                b = ps_x[use % 2]
                if of_q:
                    dve.wait_ge(qk_cast, 4 * j + use + 1)
                    dve.tensor_tensor(qB[par][p][0:DK, c], b[0:DK, :], qA[par][p][0:DK, c].bitcast(F32), ALU.subtract)
                else:
                    dve.tensor_tensor(kA[par][p][0:DK, c], b[DK:P, :], kA[par][p][DK:P, c].bitcast(F32),
                                      ALU.subtract).then_inc(qk_low, 1)

            def reduce_max(j, m):
                p, qt, kh = m // 16, (m // 2) % 8, m % 2
                dve.wait_ge(m_done, UNITS * j + m + 1)
                dve.tensor_reduce(mxp[p][:, qt, kh:kh + 1], ps_m[m % 2][:, :], AX_X, ALU.max).then_inc(maxed, 1)
                if m % 16 == 15:
                    dve.wait_ge(maxed, UNITS * j + m + 1)
                    dve.tensor_reduce(mxw[p][:, DK:KB], mxp[p][:, :, :], AX_X, ALU.max).then_inc(mx_ready, 1)

            def place_max(j, par, p):
                dve.wait_ge(c_done, 2 * j + p + 1)
                rows = ps_x[p][DK:KB, 0:P].rearrange("r (o q) -> r o q", o=1).to_broadcast([NB, QT, P])
                dve.tensor_tensor(qB[par][p][DK:KB, :].rearrange("r (t q) -> r t q", q=P), rows,
                                  rowmask[DK:KB, :].rearrange("r (t q) -> r t q", q=P), ALU.mult).then_inc(c_placed, 1)

            def recip(j, half, quarter):
                c = half * HALF + quarter * P
                if quarter == 0:
                    dve.wait_ge(sums_done, 2 * j + half + 1)
                dve.reciprocal(rc[:, c:c + P], ps_x[half][:, quarter * P:(quarter + 1) * P]).then_inc(recip_done, 1)
                if quarter == 3:
                    dve.wait_ge(recip_done, 8 * j + 4 * half + 4)
                    dve.wait_ge(z_copied, 2 * j + half + 1)
                    d = slice(half * HALF, (half + 1) * HALF)
                    dve.tensor_tensor(zT[:, d], zr[:, d], rc[:, d], ALU.mult).then_inc(z_ready, 1)

            def add_wo(j, g):
                dve.wait_ge(wo_done, 2 * j + g + 1)
                at = x2[:, bass.ds((j // HP) * S + g * HALF, HALF)]
                dve.tensor_tensor(at, ps_x[g][:, :], at, ALU.add).then_inc(wo_added, 1)

            def pair(j, par, first=False, second=False, last=False):
                for u in range(UNITS + 1):
                    if not last and u - 1 in C_AT:
                        place_max(j + 1, 1 - par, C_AT[u - 1])
                    if not last:
                        for m in max_units(u):
                            reduce_max(j + 1, m)
                        if u - LOW_Q in QK_AT:
                            low_qk(j + 1, 1 - par, QK_AT[u - LOW_Q], True)
                        if u - LOW_K in QK_AT:
                            low_qk(j + 1, 1 - par, QK_AT[u - LOW_K], False)
                    if not (first or second) and u - 1 in WO_AT:
                        add_wo(j - 2, WO_AT[u - 1])
                    if not first and u in RECIP_AT:
                        recip(j - 1, *RECIP_AT[u])

            for use in range(4):
                low_qk(0, 0, use, True)
                low_qk(0, 0, use, False)
            for m in range(UNITS):
                reduce_max(0, m)
            for p in range(2):
                place_max(0, 0, p)
            dve.wait_ge(residual_ready, B)
            pair(0, 0, first=True)
            pair(1, 1, second=True)
            with dve.Fori(0, PAIR_LOOP) as i:
                for par in range(2):
                    pair(2 * i + 2 + par, par)
            pair(PAIRS - 2, 0)
            pair(PAIRS - 1, 1, last=True)
            for g in range(2):
                add_wo(PAIRS - 2, g)
            for n in range(8):
                recip(PAIRS - 1, *divmod(n, 4))
            for g in range(2):
                add_wo(PAIRS - 1, g)

            dve.wait_ge(wo_added, 2 * PAIRS)
            for b in range(B):
                norm(B + b, b)

            def wide(a):
                return a.rearrange("p (t o) -> p t o", o=1).to_broadcast([P, TT, E])

            top, total, prob, first_e, rank, keep, slot, a_, b_, c_, w_ = (cols[:, k, :] for k in range(11))
            dve.wait_ge(logits_done, 1)
            dve.wait_ge(consts, 5)
            then(dve.tensor_copy(lg, ps_m[0][:, 0:TT * E].rearrange("p (t e) -> p t e", e=E)))
            then(dve.tensor_reduce(top, lg, AX_X, ALU.max))
            dve.tensor_tensor(ex, lg, wide(top), ALU.subtract).then_inc(shifted, 1)
            then(dve.tensor_tensor(hot, lg, wide(top), ALU.is_equal))
            then(dve.scalar_tensor_tensor(out=cand, in0=hot, scalar=-float(E), in1=iota_e, op0=ALU.mult, op1=ALU.add))
            then(dve.tensor_reduce(first_e, cand, AX_X, ALU.min))
            then(dve.tensor_tensor(hot, cand, wide(first_e), ALU.is_equal))
            dve.tensor_copy(hot_b[:, :].rearrange("p (t e) -> p t e", e=E), hot).then_inc(onehot_ready, 1)
            dve.wait_ge(route_exp, 1)
            then(dve.tensor_reduce(total, ex, AX_X, ALU.add))
            then(dve.reciprocal(prob, total))
            dve.wait_ge(ranks_done, 1)
            then(dve.tensor_tensor(ex, hot, ps_m[1][:, 0:TT * E].rearrange("p (t e) -> p t e", e=E), ALU.mult))
            then(dve.tensor_reduce(rank, ex, AX_X, ALU.add))
            then(dve.tensor_scalar(keep, rank, float(CAP), None, ALU.is_lt))
            then(dve.tensor_tensor(w_, keep, prob, ALU.mult))
            then(dve.tensor_scalar(a_, first_e, float(E), float(CAP), ALU.add, ALU.mult))
            then(dve.tensor_tensor(slot, a_, rank, ALU.add))
            then(dve.tensor_tensor(b_, slot, token_no[:, :], ALU.subtract))
            then(dve.tensor_scalar(a_, b_, -float(E * CAP), None, ALU.add))
            then(dve.tensor_tensor(b_, a_, keep, ALU.mult))
            then(dve.tensor_tensor(a_, b_, token_no[:, :], ALU.add))
            then(dve.tensor_scalar(c_, a_, float(E * CAP), None, ALU.add))
            then(dve.tensor_copy(scatter_at[:, :], c_))
            dve.tensor_scalar(gather_at[:, :], c_, float(E * CAP - 1), None, ALU.min).then_inc(index_ready, 1)

            for e in range(E):
                if e >= 2:
                    dve.wait_ge(down_done, e - 1)
                for c in range(FC):
                    n = e * FC + c
                    dve.wait_ge(up_done, n + 1)
                    dve.tensor_scalar(rT[e % 2][:, c * HALF:(c + 1) * HALF], ps_s[n % 2][:, :], 0.0, None,
                                      ALU.max).then_inc(relu_done, 1)
            for t in range(TT):
                dve.wait_ge(gathered, 16 * TT)
                at = x2[:, t * D:(t + 1) * D]
                dve.scalar_tensor_tensor(out=at, in0=yg[:, t * D:(t + 1) * D], scalar=w_[:, t:t + 1], in1=at,
                                         op0=ALU.mult, op1=ALU.add).then_inc(out_ready, 1)

        @block.tensor
        def _(pe):
            pe.wait_ge(consts, 5)
            pe.wait_ge(dve_consts, 12)
            for b in range(B):
                pe.wait_ge(h_ready, b + 1)
                for g in range(2):
                    n = 2 * b + g
                    if n >= 2:
                        pe.wait_ge(hT_ready, n - 1)
                    for i in range(4):
                        t = 4 * g + i
                        mm = pe.transpose(ps_x[g][:, i * P:(i + 1) * P], h_tok(b)[:, t * D:(t + 1) * D], ident[:, :])
                    mm.then_inc(h_turned, 1)

            def project_qk(j, par, use):
                p, half = divmod(use, 2)
                if use == 0:
                    pe.wait_ge(w_loaded[par], 64 * (j // 2) + 64)
                pe.matmul(ps_x[use % 2][:, :], wst[par][:, p * P:(p + 1) * P],
                          hTs[par][:, half * HALF:(half + 1) * HALF], start=True, stop=True).then_inc(qk_done, 1)

            def project_v(j, par, half):
                pe.wait_ge(qk_low, 4 * j + 2 + half + 1)
                for i in range(4):
                    t = 4 * half + i
                    mm = pe.matmul(ps_x[half][:, i * P:(i + 1) * P], hTs[par][:, t * P:(t + 1) * P],
                                   wst[par][:, 4 * DK:6 * DK], start=True, stop=True)
                mm.then_inc(v_done, 1)

            def max_scores(j, par, m):
                p, qt, kh = m // 16, (m // 2) % 8, m % 2
                if m % 16 == 0:
                    pe.wait_ge(qk_low, 4 * j + 2 * p + 2)
                    pe.wait_ge(qk_cast_again, 4 * j + 2 * p + 2)
                if not (isinstance(j, int) and j == 0 and m < 2):
                    pe.wait_ge(maxed, UNITS * j + m - 1)
                pe.matmul(ps_m[m % 2][:, :], qA[par][p][:, qt * P:(qt + 1) * P],
                          kA[par][p][:, kh * HALF:(kh + 1) * HALF], start=True, stop=True).then_inc(m_done, 1)

            def turn_max(j, p):
                pe.wait_ge(mx_ready, 2 * j + p + 1)
                pe.transpose(ps_x[p][0:KB, 0:P], mxw[p][:, :], ident[:, :]).then_inc(c_done, 1)

            def scores(j, par, u):
                kt, half, p = u // 4, (u // 2) % 2, u % 2
                if u < 2:
                    pe.wait_ge(c_placed, 2 * j + u + 1)
                if not (isinstance(j, int) and j == 0 and u < 2):
                    pe.wait_ge(exp_done, UNITS * j + u - 1)
                c = slice(half * HALF, (half + 1) * HALF)
                k = slice(kt * P, (kt + 1) * P)
                pe.matmul(ps_s[u % 2][:, :], kA[par][p][:, k], qA[par][p][:, c], start=True, stop=False)
                pe.matmul(ps_s[u % 2][:, :], kB[par][p][:, k], qB[par][p][:, c], start=False,
                          stop=True).then_inc(scores_ready, 1)

            def values(j, par, kt, half, first=False):
                if kt == 0:
                    pe.wait_ge(v_copied, 2 * j + 2)
                    if not first:
                        pe.wait_ge(z_copied, 2 * j - 1 + half)
                for p in range(2):
                    mm = pe.matmul(ps_z[half][p * DK:(p + 1) * DK, :],
                                   V[par][:, kt * P + p * DK:kt * P + (p + 1) * DK], P_tile(kt, p, half),
                                   start=(kt == 0), stop=(kt == KT - 1))
                mm.then_inc(pv_done, 1)

            def softmax_sums(j, par, half):
                pe.wait_ge(summed, 14 * j + 14)
                for p in range(2):
                    at = p * S + half * HALF
                    mm = pe.matmul(ps_x[half][p * DK:(p + 1) * DK, :], ones[:, :], acc[par][:, at:at + HALF],
                                   start=True, stop=True)
                mm.then_inc(sums_done, 1)

            def project_out(j, par, g):
                pe.wait_ge(wo_loaded[par], 16 * (j // 2) + 16)
                pe.wait_ge(z_ready, 2 * j + g + 1)
                for i in range(4):
                    t = 4 * g + i
                    mm = pe.matmul(ps_x[g][:, i * P:(i + 1) * P], zT[:, t * P:(t + 1) * P], wo[par][:, :],
                                   start=True, stop=True)
                mm.then_inc(wo_done, 1)

            def pair(j, par, first=False, second=False, last=False):
                nxt = 1 - par
                for u in range(UNITS):
                    kt, odd = u // 4, u % 4
                    scores(j, par, u)
                    ms = list(max_units(u)) if not last else []
                    for m in ms[:1]:
                        max_scores(j + 1, nxt, m)
                    if odd in (1, 3) and (kt > 0 or not first):
                        half = odd // 2
                        if kt > 0:
                            values(j, par, kt - 1, half, first)
                        else:
                            values(j - 1, nxt, KT - 1, half, second)
                    if not last and u in QK_AT:
                        use = QK_AT[u]
                        if use >= 2:
                            pe.wait_ge(qk_low, 4 * (j + 1) + use - 1)
                        elif first or second:
                            pe.wait_ge(c_placed, 2 * j + use + 1)
                        else:
                            pe.wait_ge(recip_done, 8 * (j - 2) + 4 * use + 4)
                        project_qk(j + 1, nxt, use)
                    if not last and u in V_AT:
                        project_v(j + 1, nxt, V_AT[u])
                    if not (first or second) and u in WO_AT:
                        if last:
                            pe.wait_ge(recip_done, 8 * (j - 2) + 4 * WO_AT[u] + 4)
                        else:
                            pe.wait_ge(v_copied, 2 * (j + 1) + WO_AT[u] + 1)
                        project_out(j - 2, par, WO_AT[u])
                    if not last and u in C_AT:
                        p = C_AT[u]
                        if first or second:
                            pe.wait_ge(v_copied, 2 * (j + 1) + p + 1)
                        else:
                            pe.wait_ge(wo_added, 2 * (j - 2) + p + 1)
                        turn_max(j + 1, p)
                    if not first and u in SUM_AT:
                        half = SUM_AT[u]
                        if last:
                            pe.wait_ge(wo_added, 2 * (j - 2) + half + 1)
                        else:
                            pe.wait_ge(c_placed, 2 * (j + 1) + half + 1)
                        softmax_sums(j - 1, nxt, half)
                    for m in ms[1:]:
                        max_scores(j + 1, nxt, m)

            for use in range(4):
                if use < 2:
                    pe.wait_ge(hT_ready, 2 * B)
                else:
                    pe.wait_ge(qk_low, use - 1)
                project_qk(0, 0, use)
            for half in range(2):
                project_v(0, 0, half)
            for m in range(UNITS):
                max_scores(0, 0, m)
            for p in range(2):
                pe.wait_ge(v_copied, p + 1)
                turn_max(0, p)
            pair(0, 0, first=True)
            pair(1, 1, second=True)
            with pe.Fori(0, PAIR_LOOP) as i:
                for par in range(2):
                    pair(2 * i + 2 + par, par)
            pair(PAIRS - 2, 0)
            last = PAIRS - 1
            pair(last, 1, last=True)
            pe.wait_ge(exp_done, UNITS * PAIRS)
            for half in range(2):
                values(last, 1, KT - 1, half)
            for g in range(2):
                pe.wait_ge(recip_done, 8 * (last - 1) + 4 * g + 4)
                project_out(last - 1, 0, g)
            for half in range(2):
                pe.wait_ge(wo_added, 2 * (last - 1) + half + 1)
                softmax_sums(last, 1, half)
            for g in range(2):
                project_out(last, 1, g)

            pe.wait_ge(wo_added, 2 * PAIRS)
            for n in range(2 * B):
                pe.wait_ge(h_ready, B + n // 2 + 1)
                if n >= 2:
                    pe.wait_ge(h2T_ready, n - 1)
                for i in range(4):
                    t = 4 * n + i
                    mm = pe.transpose(ps_x[n % 2][:, i * P:(i + 1) * P], ring[:, t * D:(t + 1) * D], ident[:, :])
                mm.then_inc(h2_turned, 1)
            pe.wait_ge(wr_loaded, 16)
            pe.wait_ge(h2T_ready, 2 * B)
            for t in range(TT):
                mm = pe.matmul(ps_m[0][:, t * E:(t + 1) * E], h2T[:, t * P:(t + 1) * P], wr[:, :],
                               start=True, stop=True)
            mm.then_inc(logits_done, 1)
            pe.wait_ge(onehot_ready, 1)
            for t in range(TT - 1):
                left = TT - 1 - t
                pe.matmul(ps_m[1][:, (t + 1) * E:TT * E].rearrange("p (t e) -> p t e", e=E), ones_b[:, :],
                               hot_b[:, t * E:(t + 1) * E].rearrange("p (o e) -> p o e", o=1).to_broadcast([P, left, E]),
                          start=(t == 0), stop=False, skip_group_check=True)
            pe.matmul(ps_m[1][:, 0:TT * E], upper[:, :], hot_b[:, :], start=False, stop=True,
                      skip_group_check=True).then_inc(ranks_done, 1)

            def turn_tokens(e):
                pe.wait_ge(xe_loaded[e % 2], 16 * (e // 2 + 1))
                if e >= 2:
                    pe.wait_ge(xeT_ready, e - 1)
                for i in range(ST):
                    mm = pe.transpose(ps_x[e % 2][:, i * P:(i + 1) * P], xe[e % 2][:, i * D:(i + 1) * D],
                                      ident[:, :])
                mm.then_inc(xe_turned, 1)

            def down(e):
                if e >= 2:
                    pe.wait_ge(ye_copied, e - 1)
                pe.wait_ge(relu_done, FC * (e + 1))
                for st in range(ST):
                    for c in range(FC):
                        mm = pe.matmul(ps_z[e % 2][:, st * P:(st + 1) * P],
                                       rT[e % 2][:, c * HALF + st * P:c * HALF + (st + 1) * P],
                                       w2_sb[:, (c * E + e) * D:(c * E + e + 1) * D], start=(c == 0), stop=(c == FC - 1))
                mm.then_inc(down_done, 1)

            pe.wait_ge(w1_loaded, 16)
            pe.wait_ge(w2_loaded, 16 * FC)
            turn_tokens(0)
            for e in range(E):
                if e + 1 < E:
                    turn_tokens(e + 1)
                pe.wait_ge(xeT_ready, e + 1)
                for c in range(FC):
                    n = e * FC + c
                    if n >= 2:
                        pe.wait_ge(relu_done, n - 1)
                    pe.matmul(ps_s[n % 2][:, :], w1_sb[:, e * F + c * P:e * F + (c + 1) * P],
                              xeT[e % 2][:, :], start=True, stop=True).then_inc(up_done, 1)
                if e >= 1:
                    down(e - 1)
            down(E - 1)


_INS = ["L0_attn_x", "L0_attn_w_q", "L0_attn_w_k", "L0_attn_w_v", "L0_attn_w_o", "L0_ffn_Wr", "L0_ffn_W1", "L0_ffn_W2"]


def kernel(**inputs):
    import numpy as _np
    import concourse.bacc as _bacc
    from concourse import mybir as _mybir
    from concourse.bass_utils import run_bass_kernel_spmd as _run

    nc = _bacc.Bacc("TRN2", target_bir_lowering=False, num_devices=1)
    arrays, args = {}, []
    for name in _INS:
        a = _np.ascontiguousarray(inputs[name])
        arrays[f"in_{name}"] = a
        args.append(nc.dram_tensor(f"in_{name}", a.shape, _mybir.dt.from_np(a.dtype), kind="ExternalInput").ap())
    shape = inputs["L0_attn_x"].shape
    args.append(nc.dram_tensor("out_0", shape, _mybir.dt.float32, kind="ExternalOutput").ap())
    block_kernel(nc, *args)
    r = _run(nc, [arrays], core_ids=[0])
    return r.results[0]["out_0"]
```

```python
from contextlib import ExitStack

import concourse.bass as bass
from concourse import mybir

F32 = mybir.dt.float32
F32R = mybir.dt.float32r
I32 = mybir.dt.int32
U32 = mybir.dt.uint32
BF16 = mybir.dt.bfloat16
ALU = mybir.AluOpType
ACT = mybir.ActivationFunctionType
AX_X = mybir.AxisListType.X

P = 128
HALF = 512
EPS = 1e-5

QK_AT = {0: 0, 1: 1, 4: 2, 6: 3}
V_AT = {8: 0, 9: 1}
C_AT = {17: 0, 25: 1}
SUM_AT = {24: 0, 28: 1}
RECIP_AT = {25: (0, 0), 26: (0, 1), 27: (0, 2), 28: (0, 3), 29: (1, 0), 30: (1, 1), 31: (1, 2), 32: (1, 3)}
WO_AT = {14: 0, 19: 1}
MAX_FROM, MAX_TO = 4, 25
UNITS = 32
LOW_Q, LOW_K = 1, 2
Z_AT = {3: 0, 4: 1}

STATS_AT = 1
NORM_AT = 10
TURN_AT = {11: 0, 12: 1}
SUM_COPY_AT = {15: 0, 16: 1}
LOGITS_AT = 20
SHARE_AT = 22
RANKS_AT = 23

EARLY_TURN_AT = [{11: (1, 0), 12: (1, 1), 20: (2, 0), 21: (2, 1)}, {11: (3, 0), 12: (3, 1)}]
RESIDUAL_AFTER = 4


def max_units(u):
    def before(v):
        return UNITS * min(max(v - MAX_FROM, 0), MAX_TO - MAX_FROM) // (MAX_TO - MAX_FROM)
    return range(before(u), before(u + 1))


def block_kernel(nc, x_in, w_q, w_k, w_v, w_o, w_r, w_1, w_2, out):
    B, S, D = x_in.shape
    H, _, DK = w_q.shape
    E, _, F = w_1.shape
    T = B * S
    TT = T // P
    QT = S // P
    KT = S // P
    PAIRS = B * H // 2
    HP = H // 2
    CAP = -(-T // E)
    FC = F // P
    ST = CAP // P
    SCALE = 1.0 / float(DK) ** 0.5
    NB = 8
    KB = DK + NB
    RING = 4
    assert D == P and 2 * DK == P and 2 * HALF == S and QT == NB and CAP == HALF and PAIRS % 2 == 0
    assert UNITS == 4 * KT

    x_t = x_in.rearrange("b (n p) d -> b p n d", p=P)
    out_t = out.rearrange("b (n p) d -> b p n d", p=P)
    wq_d = w_q.rearrange("h d k -> d h k")
    wk_d = w_k.rearrange("h d k -> d h k")
    wv_d = w_v.rearrange("h d k -> d h k")
    wo_d = w_o.rearrange("(h p) d -> p h d", p=P)
    W = 2 * D + 2
    slots_d = nc.dram_tensor("tokens_by_slot", (E * CAP, W), F32, kind="Internal").ap()
    out_rows = out.rearrange("b s d -> (b s) d")

    with ExitStack() as ctx:
        def sb(name, shape, dt=F32):
            return ctx.enter_context(nc.sbuf_tensor(name, shape, dt))

        def sem(name):
            return ctx.enter_context(nc.semaphore(name))

        x2 = sb("x2", [P, TT * D])
        ring = sb("ring", [P, RING * 2 * S])
        ident = sb("ident", [P, P])
        upper = sb("upper", [P, P], BF16)
        ones_b = sb("ones_b", [P, P], BF16)
        moments = sb("moments", [P, 2 * B, QT, 2])
        moment_parts = sb("moment_parts", [P, QT, 6])
        roots = sb("roots", [P, 2 * B, 3, QT])
        rows = sb("rows", [P, QT, W])
        h2T = sb("h2T", [P, S])
        wr = sb("wr", [P, E])
        lg, ex, hot, cand = (sb(n, [P, TT * E])[:, :].rearrange("p (t e) -> p t e", e=E)
                             for n in ("logits", "shifted_logits", "one_hot", "candidate"))
        iota_e = sb("expert_no", [P, QT * E])[:, :].rearrange("p (t e) -> p t e", e=E)
        hot_b = sb("one_hot_b", [P, B, (QT + 1) * E], BF16)
        seen = sb("seen", [P, B + 1, E])
        cols = sb("routing_columns", [P, 6, TT])
        scatter_at = sb("scatter_at", [P, TT], I32)

        with ExitStack() as later:
            def sb_later(name, shape):
                return later.enter_context(nc.sbuf_tensor(name, shape, F32))

            w1_sb = sb_later("w1", [P, E * F])
            w2_sb = sb_later("w2", [P, FC * E * D])
            xeT = [sb_later(f"xeT{i}", [P, HALF]) for i in range(2)]
            rT = [sb_later(f"rT{i}", [P, FC * HALF]) for i in range(2)]
            ye = [sb_later(f"ye{i}", [P, HALF]) for i in range(2)]

        kA = [[sb(f"kA{i}{p}", [P, S], F32R) for p in range(2)] for i in range(2)]
        qA = [[sb(f"qA{i}{p}", [P, S], F32R) for p in range(2)] for i in range(2)]
        kB = [[sb(f"kB{i}{p}", [KB, S], F32R) for p in range(2)] for i in range(2)]
        qB = [[sb(f"qB{i}{p}", [KB, S], F32R) for p in range(2)] for i in range(2)]
        hT = sb("hT", [P, T])
        hTs = [sb(f"hTs{i}", [P, S]) for i in range(2)]
        wst = [sb(f"wst{i}", [P, 6 * DK]) for i in range(2)]
        wo = [sb(f"wo{i}", [P, D]) for i in range(2)]
        V = [sb(f"V{i}", [P, KT * P]) for i in range(2)]
        acc = [sb(f"acc{i}", [P, 2 * S]) for i in range(2)]
        zr = sb("zr", [P, S])
        zT = sb("zT", [P, S])
        rc = sb("rc", [P, S])
        mxp = [sb(f"mxp{p}", [P, QT, 2]) for p in range(2)]
        mxw = [sb(f"mxw{p}", [P, KB]) for p in range(2)]
        rowmask = sb("rowmask", [KB, S])
        ones = sb("ones", [P, DK])

        XE = min(E, RING * 2 * S // (ST * W))
        def xe(e):
            at = (e % XE) * ST * W
            return ring[:, at:at + ST * W].rearrange("p (n w) -> p n w", w=W)

        def P_tile(kt, p, half):
            at = ((kt % RING) * 2 + p) * S + half * HALF
            return ring[:, at:at + HALF]

        ps_s = [ctx.enter_context(nc.psum_tensor(f"ps_s{i}", [P, HALF], F32)) for i in range(2)]
        ps_m = [ctx.enter_context(nc.psum_tensor(f"ps_m{i}", [P, HALF], F32)) for i in range(2)]
        ps_z = [ctx.enter_context(nc.psum_tensor(f"ps_z{i}", [P, HALF], F32)) for i in range(2)]
        ps_x = [ctx.enter_context(nc.psum_tensor(f"ps_x{i}", [P, HALF], F32)) for i in range(2)]

        x_loaded = [sem(f"x_loaded{b}") for b in range(B)]
        w_loaded = [sem(f"w_loaded{i}") for i in range(2)]
        wo_loaded = [sem(f"wo_loaded{i}") for i in range(2)]
        wr_loaded = sem("wr_loaded")
        consts = sem("consts")
        dve_consts = sem("dve_consts")
        chain = sem("chain")
        moments_ready = sem("moments_ready")
        root_ready = sem("root_ready")
        root_chain = sem("root_chain")
        h_ready = sem("h_ready")
        residual_ready = sem("residual_ready")
        h_turned = sem("h_turned")
        hT_ready = sem("hT_ready")

        qk_done = sem("qk_done")
        qk_cast = sem("qk_cast")
        qk_cast_again = sem("qk_cast_again")
        qk_low = sem("qk_low")
        v_done = sem("v_done")
        v_copied = sem("v_copied")
        m_done = sem("m_done")
        maxed = sem("maxed")
        mx_ready = sem("mx_ready")
        c_done = sem("c_done")
        c_placed = sem("c_placed")
        scores_ready = sem("scores_ready")
        exp_done = sem("exp_done")
        pv_done = sem("pv_done")
        summed = sem("summed")
        sums_done = sem("sums_done")
        z_copied = sem("z_copied")
        recip_done = sem("recip_done")
        z_ready = sem("z_ready")
        wo_done = sem("wo_done")
        wo_added = sem("wo_added")

        rows_cleared = sem("rows_cleared")
        row_numbers = sem("row_numbers")
        slots_cleared = sem("slots_cleared")
        w1_loaded = sem("w1_loaded")
        w2_loaded = sem("w2_loaded")
        h2_ready = sem("h2_ready")
        sum_copied = sem("sum_copied")
        h2_turned = sem("h2_turned")
        h2T_ready = sem("h2T_ready")
        logits_done = sem("logits_done")
        shifted = sem("shifted")
        route_exp = sem("route_exp")
        onehot_ready = sem("onehot_ready")
        ranks_done = sem("ranks_done")
        index_ready = sem("index_ready")
        scattered = [sem(f"scattered{b}") for b in range(B)]
        residual_stored = sem("residual_stored")
        xe_loaded = [sem(f"xe_loaded{i}") for i in range(XE)]
        xe_turned = sem("xe_turned")
        xeT_ready = sem("xeT_ready")
        up_done = sem("up_done")
        relu_done = sem("relu_done")
        down_done = sem("down_done")
        ye_ready = sem("ye_ready")
        stored = [sem(f"stored{i}") for i in range(2)]

        def h_tok(b):
            return rows[:, :, (b % 2) * D:(b % 2 + 1) * D]

        block = ctx.enter_context(nc.Block())

        PAIR_LOOP = (PAIRS - 6) // 2
        LAST_BY_PE = 2
        ROUTE_FROM = PAIRS - 4
        assert 8 * (B - 1) + 2 <= ROUTE_FROM + B - 2 and PAIRS - 1 - ROUTE_FROM == B - 1

        @block.sync
        def _(sp):
            for b in range(B):
                sp.dma_start(x2[:, b * S:(b + 1) * S].rearrange("p (n d) -> p n d", d=D),
                             x_t[b]).then_inc(x_loaded[b], 16)
            sp.dma_start(wr[:, :], w_r).then_inc(wr_loaded, 16)

            def load_weights(j, par):
                hp, b = j % HP, j // HP
                view = wst[par][:, 0:4 * DK].rearrange("p (h t k) -> p h t k", h=2, t=2)
                sp.dma_start(view[:, :, 0, :], wq_d[:, bass.ds(2 * hp, 2), :]).then_inc(w_loaded[par], 16)
                sp.dma_start(view[:, :, 1, :], wk_d[:, bass.ds(2 * hp, 2), :]).then_inc(w_loaded[par], 16)
                sp.dma_start(wst[par][:, 4 * DK:6 * DK].rearrange("p (h k) -> p h k", h=2),
                             wv_d[:, bass.ds(2 * hp, 2), :]).then_inc(w_loaded[par], 16)
                if not (isinstance(j, int) and j == 0):
                    sp.wait_ge(hT_ready, 2 * b + 2)
                    sp.dma_start(hTs[par][:, :], hT[:, bass.ds(b * S, S)]).then_inc(w_loaded[par], 16)

            def load_wo(j, par):
                sp.dma_start(wo[par][:, :].rearrange("p (o d) -> p o d", o=1),
                             wo_d[:, bass.ds(j % HP, 1), :]).then_inc(wo_loaded[par], 16)

            for j in range(2):
                load_weights(j, j)
                load_wo(j, j)
            def loads(j, par):
                sp.wait_ge(v_done, 2 * j - 2)
                load_weights(j, par)
                sp.wait_ge(wo_done, 2 * j - 4)
                load_wo(j - 1, 1 - par)

            sp.wait_ge(v_done, 2)
            load_weights(2, 0)
            loads(3, 1)
            sp.wait_ge(rows_cleared, 2)
            for n in range(E * CAP // S):
                sp.dma_start(slots_d[n * S:(n + 1) * S, :].rearrange("(p n) w -> p n w", p=P),
                             rows[:, :, :]).then_inc(slots_cleared, 16)

            with sp.Fori(0, PAIR_LOOP - 1) as i:
                for par in range(2):
                    loads(2 * i + 4 + par, par)
            for j in range(2 * PAIR_LOOP + 2, PAIRS):
                loads(j, j % 2)
            sp.wait_ge(wo_done, 2 * PAIRS - 4)
            load_wo(PAIRS - 1, (PAIRS - 1) % 2)

            sp.wait_ge(scores_ready, UNITS * PAIRS)
            sp.dma_start(w1_sb[:, :].rearrange("p (e f) -> p e f", e=E),
                         w_1.rearrange("e d f -> d e f")).then_inc(w1_loaded, 16)
            for c in range(FC):
                sp.dma_start(w2_sb[:, c * E * D:(c + 1) * E * D].rearrange("p (e d) -> p e d", e=E),
                             w_2.rearrange("e (c p) d -> c p e d", p=P)[c]).then_inc(w2_loaded, 16)

            for b in range(B):
                sp.wait_ge(wo_added, 2 * HP * (b + 1))
                sp.dma_start(out_t[b], x2[:, b * S:(b + 1) * S].rearrange("p (n d) -> p n d", d=D)
                             ).then_inc(residual_stored, 16)

            for b in range(B):
                sp.wait_ge(scattered[b], 16 * QT)
            for e in range(E):
                if e >= XE:
                    sp.wait_ge(stored[(e - XE) % 2], 16 * ST * ((e - XE) // 2 + 1))
                sp.dma_start(xe(e), slots_d[e * CAP:(e + 1) * CAP, :].rearrange("(n p) w -> p n w", p=P)
                             ).then_inc(xe_loaded[e % XE], 16)
            for i in range(2):
                sp.wait_ge(stored[i], 16 * ST * E // 2)

        @block.gpsimd
        def _(pool):
            pool.wait_ge(dve_consts, 3)
            pool.affine_select(out=ident[:, :], in_=ident[:, :], compare_op=ALU.is_equal, fill=0.0,
                               base=0, pattern=[[-1, P]], channel_multiplier=1).then_inc(consts, 1)
            pool.affine_select(out=rowmask[:, :].rearrange("p (t q) -> p t q", q=P),
                               in_=rowmask[:, :].rearrange("p (t q) -> p t q", q=P),
                               compare_op=ALU.is_equal, fill=0.0, base=-DK,
                               pattern=[[-1, NB], [0, P]], channel_multiplier=1).then_inc(consts, 1)
            pool.affine_select(out=upper[:, :], in_=upper[:, :], compare_op=ALU.is_gt, fill=0.0,
                               base=0, pattern=[[1, P]], channel_multiplier=-1).then_inc(consts, 1)
            pool.iota(iota_e, pattern=[[0, QT], [1, E]], base=0, channel_multiplier=0,
                      allow_small_or_imprecise_dtypes=True).then_inc(consts, 1)

            steps = [0]

            def then(ins):
                steps[0] += 1
                ins.then_inc(root_chain, 1)
                pool.wait_ge(root_chain, steps[0])

            def inverse_root(n):
                v, y, t = (roots[:, n, k, :] for k in range(3))
                pool.wait_ge(moments_ready, n + 1)
                then(pool.tensor_scalar(v, moments[:, n, :, 1], EPS, None, ALU.add))
                then(pool.tensor_scalar(y.bitcast(I32), v.bitcast(I32), -0.5, float(0x5F3759DF), ALU.mult, ALU.add))
                for step in range(4):
                    then(pool.tensor_tensor(t, y, y, ALU.mult))
                    then(pool.tensor_tensor(t, t, v, ALU.mult))
                    then(pool.tensor_scalar(t, t, -0.5, 1.5, ALU.mult, ALU.add))
                    if step < 3:
                        then(pool.tensor_tensor(y, y, t, ALU.mult))
                pool.tensor_tensor(y, y, t, ALU.mult).then_inc(root_ready, 1)

            def residual(b):
                pool.wait_ge(h_ready, b + 1)
                at = x2[:, b * S:(b + 1) * S].rearrange("p (t d) -> p t d", d=D)
                pool.tensor_tensor(at, at, h_tok(b), ALU.add).then_inc(residual_ready, 1)

            for b in range(2):
                inverse_root(b)
            for b in range(2):
                residual(b)

            def number_rows(b):
                if b == 0:
                    pool.wait_ge(slots_cleared, 16 * (E * CAP // S))
                else:
                    pool.wait_ge(scattered[b - 1], 16 * QT)
                pool.iota(rows[:, :, W - 1].bitcast(I32), pattern=[[P, QT]], base=b * S,
                          channel_multiplier=1).then_inc(row_numbers, 1)

            def scatter(b):
                pool.wait_ge(row_numbers, b + 1)
                pool.wait_ge(index_ready, b + 1)
                pool.wait_ge(sum_copied, 2 * b + 2)
                for t in range(QT):
                    i = b * QT + t
                    pool.indirect_dma_start(
                        out=slots_d, in_=rows[:, t, :], in_offset=None,
                        out_offset=bass.IndirectOffsetOnAxis(ap=scatter_at[:, i:i + 1].bitcast(U32), axis=0),
                        bounds_check=E * CAP - 1, oob_is_err=False).then_inc(scattered[b], 16)

            def add_up(j, par, early=None, routes=None, upto=KT):
                if routes is not None:
                    inverse_root(B + routes)
                    number_rows(routes)
                if early is not None:
                    inverse_root(early)
                for kt in range(1, upto):
                    if early is not None and kt == RESIDUAL_AFTER + 1:
                        residual(early)
                    if routes is not None and kt == KT - 1:
                        scatter(routes)
                    for p in range(2):
                        a = acc[par][:, p * S:(p + 1) * S]
                        n = 2 * (kt - 1) + p
                        pool.wait_ge(exp_done, UNITS * j + 4 * kt + 3 + p)
                        if kt > 1:
                            pool.wait_ge(summed, 14 * j + n - 1)
                        before = a if kt > 1 else ring[:, p * S:(p + 1) * S]
                        now = ring[:, ((kt % RING) * 2 + p) * S:((kt % RING) * 2 + p + 1) * S]
                        pool.tensor_tensor(a, before, now, ALU.add).then_inc(summed, 1)

            for j in range(2):
                add_up(j, j, early=2 + j)
            with pool.Fori(0, ROUTE_FROM // 2 - 1) as i:
                for par in range(2):
                    add_up(2 * i + 2 + par, par)
            for b in range(B - 1):
                add_up(ROUTE_FROM + b, b % 2, routes=b)
            add_up(PAIRS - 1, 1, upto=KT - LAST_BY_PE)
            inverse_root(2 * B - 1)
            number_rows(B - 1)
            scatter(B - 1)

            pool.wait_ge(residual_stored, 16 * B)
            for e in range(E):
                for n in range(ST):
                    pool.wait_ge(ye_ready, e * ST + n + 1)
                    pool.indirect_dma_start(
                        out=out_rows, in_=ye[e % 2][:, n * D:(n + 1) * D], in_offset=None,
                        out_offset=bass.IndirectOffsetOnAxis(ap=xe(e)[:, n, W - 1:W].bitcast(U32), axis=0),
                        bounds_check=T - 1, oob_is_err=False).then_inc(stored[e % 2], 16)

        @block.scalar
        def _(act):
            def copy_turned(n, into, done, turned):
                act.wait_ge(turned, n + 1)
                act.activation(into, ps_x[n % 2][:, :], ACT.Copy).then_inc(done, 1)

            def copy_hT(b, g):
                n = 2 * b + g
                copy_turned(n, hT[:, n * HALF:(n + 1) * HALF], hT_ready, h_turned)

            for g in range(2):
                copy_hT(0, g)

            def copy_h2T(b, g):
                if b > 0:
                    act.wait_ge(logits_done, b)
                copy_turned(2 * b + g, h2T[:, g * HALF:(g + 1) * HALF], h2T_ready, h2_turned)

            def copy_sums(b, g):
                act.wait_ge(h2_ready, b + 1)
                at = b * S + g * HALF
                act.activation(rows[:, g * QT // 2:(g + 1) * QT // 2, D:2 * D],
                               x2[:, at:at + HALF].rearrange("p (t d) -> p t d", d=D), ACT.Copy).then_inc(sum_copied, 1)

            def shares(b):
                act.wait_ge(shifted, b + 1)
                e = ex[:, b * QT:(b + 1) * QT, :]
                act.activation(e, e, ACT.Exp).then_inc(route_exp, 1)

            def cast_qk(j, par, use, again):
                p, half = divmod(use, 2)
                c = slice(half * HALF, (half + 1) * HALF)
                b = ps_x[use % 2]
                if not again:
                    act.wait_ge(qk_done, 4 * j + use + 1)
                    act.activation(qA[par][p][0:DK, c], b[0:DK, :], ACT.Copy)
                    act.activation(kA[par][p][DK:P, c], b[DK:P, :], ACT.Copy).then_inc(qk_cast, 1)
                else:
                    act.wait_ge(qk_cast, 4 * j + use + 1)
                    act.activation(qA[par][p][DK:P, c], qA[par][p][0:DK, c], ACT.Copy)
                    act.activation(kB[par][p][0:DK, c], kA[par][p][DK:P, c], ACT.Copy).then_inc(qk_cast_again, 1)

            def copy_v(j, par, half):
                act.wait_ge(v_done, 2 * j + half + 1)
                act.activation(V[par][:, half * HALF:(half + 1) * HALF], ps_x[half][:, :],
                               ACT.Copy).then_inc(v_copied, 1)

            def copy_z(j, half, first=False):
                act.wait_ge(pv_done, 2 * KT * (j + 1) - 1 + half)
                if not first:
                    act.wait_ge(z_ready, 2 * j - 1 + half)
                act.activation(zr[:, half * HALF:(half + 1) * HALF], ps_z[half][:, :], ACT.Copy).then_inc(z_copied, 1)

            def unit(j, u, first):
                kt, half, p = u // 4, (u // 2) % 2, u % 2
                if not (first and kt < RING):
                    was = kt - RING if kt >= RING else kt - RING + KT
                    back = j if kt >= RING else j - 1
                    if p == 0:
                        act.wait_ge(pv_done, 2 * KT * back + 2 * was + half + 1)
                    if half == 0:
                        act.wait_ge(summed, 14 * back + 2 * (max(was, 1) - 1) + p + 1)
                act.wait_ge(scores_ready, UNITS * j + u + 1)
                act.activation(P_tile(kt, p, half), ps_s[u % 2][:, :], ACT.Exp, scale=SCALE).then_inc(exp_done, 1)

            def pair(j, par, first=False, second=False, last=False, routes=None):
                for u in range(UNITS):
                    unit(j, u, first)
                    if first or second:
                        if u in EARLY_TURN_AT[j]:
                            copy_hT(*EARLY_TURN_AT[j][u])
                    if routes is not None:
                        if u - 1 in TURN_AT:
                            copy_h2T(routes, TURN_AT[u - 1])
                        if u in SUM_COPY_AT:
                            copy_sums(routes, SUM_COPY_AT[u])
                        if u == SHARE_AT:
                            shares(routes)
                    for again in range(2):
                        if not last and u - again in QK_AT:
                            cast_qk(j + 1, 1 - par, QK_AT[u - again], again)
                    if not last and u in V_AT:
                        copy_v(j + 1, 1 - par, V_AT[u])
                    if not first and u in Z_AT:
                        copy_z(j - 1, Z_AT[u], first=second)

            for use in range(4):
                cast_qk(0, 0, use, False)
                cast_qk(0, 0, use, True)
            for half in range(2):
                copy_v(0, 0, half)
            pair(0, 0, first=True)
            pair(1, 1, second=True)
            with act.Fori(0, PAIR_LOOP) as i:
                for par in range(2):
                    pair(2 * i + 2 + par, par)
            for b in range(B - 1):
                pair(ROUTE_FROM + b, b % 2, routes=b)
            pair(PAIRS - 1, (PAIRS - 1) % 2, last=True)
            for half in range(2):
                copy_z(PAIRS - 1, half)

            for g in range(2):
                copy_h2T(B - 1, g)
            for g in range(2):
                copy_sums(B - 1, g)
            shares(B - 1)

            for e in range(E):
                act.wait_ge(xe_turned, e + 1)
                if e >= 2:
                    act.wait_ge(up_done, FC * (e - 1))
                act.activation(xeT[e % 2][:, :], ps_x[e % 2][:, :], ACT.Copy).then_inc(xeT_ready, 1)

        @block.vector
        def _(dve):
            dve.memset(ident[:, :], 1.0).then_inc(dve_consts, 1)
            dve.memset(rowmask[:, :], 1.0).then_inc(dve_consts, 1)
            dve.memset(upper[:, :], 1.0).then_inc(dve_consts, 1)
            dve.memset(hot_b[:, :, QT * E:(QT + 1) * E], 0.0).then_inc(dve_consts, 1)
            dve.memset(seen[:, 0, :], 0.0).then_inc(dve_consts, 1)
            dve.memset(ones[:, :], 1.0).then_inc(dve_consts, 1)
            dve.memset(ones_b[:, :], 1.0).then_inc(dve_consts, 1)
            for p in range(2):
                dve.memset(mxw[p][:, :], 0.0).then_inc(dve_consts, 1)
                for i in range(2):
                    dve.memset(kB[i][p][DK:KB, :].bitcast(F32), -1.0).then_inc(dve_consts, 1)
            steps = [0]

            def then(ins):
                steps[0] += 1
                ins.then_inc(chain, 1)
                dve.wait_ge(chain, steps[0])

            def find_moments(n, b):
                if n > 0:
                    dve.wait_ge(moments_ready, n)
                for t in range(QT):
                    i = b * QT + t
                    ins = dve.bn_stats(moment_parts[:, t, :], x2[:, i * D:(i + 1) * D])
                then(ins)
                for t in range(QT):
                    ins = dve.bn_aggr(moments[:, n, t, :], moment_parts[:, t, :])
                ins.then_inc(moments_ready, 1)

            def normalise(n, b, tile, done):
                dve.wait_ge(moments_ready, n + 1)
                dve.wait_ge(root_ready, n + 1)
                for t in range(QT):
                    i = b * QT + t
                    ins = dve.tensor_scalar(tile(t), x2[:, i * D:(i + 1) * D], moments[:, n, t, 0:1],
                                            roots[:, n, 1, t:t + 1], ALU.subtract, ALU.mult)
                ins.then_inc(done, 1)

            def first_moments(b):
                dve.wait_ge(x_loaded[b], 16)
                find_moments(b, b)

            def first_norm(b):
                if b >= 2:
                    dve.wait_ge(residual_ready, b - 1)
                    dve.wait_ge(h_turned, 2 * (b - 1))
                normalise(b, b, lambda t: h_tok(b)[:, t, :], h_ready)

            def clear_rows():
                dve.wait_ge(residual_ready, B)
                dve.wait_ge(h_turned, 2 * B)
                dve.memset(rows[:, :, :], 0.0).then_inc(rows_cleared, 1)
                dve.wait_ge(rows_cleared, 1)
                dve.memset(rows[:, :, W - 1].bitcast(I32), T).then_inc(rows_cleared, 1)

            for b in range(2):
                first_moments(b)
            for b in range(2):
                first_norm(b)

            def wide(a):
                return a.rearrange("p (t o) -> p t o", o=1).to_broadcast([P, QT, E])

            def of(b):
                t = slice(b * QT, (b + 1) * QT)
                return [a[:, t, :] for a in (lg, ex, hot, cand)] + [cols[:, k, t] for k in range(6)]

            def second_moments(b):
                dve.wait_ge(wo_added, 2 * HP * (b + 1))
                find_moments(B + b, b)

            def second_norm(b):
                dve.wait_ge(row_numbers, b + 1)
                normalise(B + b, b, lambda t: rows[:, t, 0:D], h2_ready)

            def choose(b):
                l, x, h, c, top, total, first_e, rank, past, slot = of(b)
                dve.wait_ge(logits_done, b + 1)
                dve.wait_ge(consts, 4)
                then(dve.tensor_copy(l, ps_x[0][:, 0:QT * E].rearrange("p (t e) -> p t e", e=E)))
                then(dve.tensor_reduce(top, l, AX_X, ALU.max))
                dve.tensor_tensor(x, l, wide(top), ALU.subtract).then_inc(shifted, 1)
                then(dve.tensor_tensor(h, l, wide(top), ALU.is_equal))
                then(dve.scalar_tensor_tensor(out=c, in0=h, scalar=-float(E), in1=iota_e, op0=ALU.mult, op1=ALU.add))
                then(dve.tensor_reduce(first_e, c, AX_X, ALU.min))
                then(dve.tensor_tensor(h, c, wide(first_e), ALU.is_equal))
                dve.tensor_copy(hot_b[:, b, 0:QT * E].rearrange("p (t e) -> p t e", e=E), h).then_inc(onehot_ready, 1)

            def find_slots(b):
                l, x, h, c, top, total, first_e, rank, past, slot = of(b)
                base = seen[:, b, :].rearrange("p (o e) -> p o e", o=1)
                made = ps_x[1][:, 0:(QT + 1) * E].rearrange("p (t e) -> p t e", e=E)
                dve.wait_ge(ranks_done, b + 1)
                then(dve.tensor_tensor(c, made[:, 0:QT, :], base.to_broadcast([P, QT, E]), ALU.add))
                dve.tensor_tensor(seen[:, b + 1:b + 2, :], made[:, QT:QT + 1, :], base, ALU.add)
                then(dve.tensor_tensor(l, h, c, ALU.mult))
                then(dve.tensor_reduce(rank, l, AX_X, ALU.add))
                dve.tensor_scalar(past, rank, float(CAP), float(E * CAP), ALU.is_ge, ALU.mult)
                then(dve.tensor_scalar(slot, first_e, float(E), float(CAP), ALU.add, ALU.mult))
                then(dve.tensor_tensor(slot, slot, rank, ALU.add))
                dve.tensor_tensor(scatter_at[:, b * QT:(b + 1) * QT], slot, past, ALU.add)
                dve.wait_ge(route_exp, b + 1)
                then(dve.tensor_reduce(total, x, AX_X, ALU.add))
                dve.reciprocal(rows[:, :, 2 * D], total).then_inc(index_ready, 1)

            def low_qk(j, par, use, of_q):
                p, half = divmod(use, 2)
                c = slice(half * HALF, (half + 1) * HALF)
                b = ps_x[use % 2]
                if of_q:
                    dve.wait_ge(qk_cast, 4 * j + use + 1)
                    dve.tensor_tensor(qB[par][p][0:DK, c], b[0:DK, :], qA[par][p][0:DK, c].bitcast(F32), ALU.subtract)
                else:
                    dve.tensor_tensor(kA[par][p][0:DK, c], b[DK:P, :], kA[par][p][DK:P, c].bitcast(F32),
                                      ALU.subtract).then_inc(qk_low, 1)

            def reduce_max(j, m):
                p, qt, kh = m // 16, (m // 2) % 8, m % 2
                dve.wait_ge(m_done, UNITS * j + m + 1)
                dve.tensor_reduce(mxp[p][:, qt, kh:kh + 1], ps_m[m % 2][:, :], AX_X, ALU.max).then_inc(maxed, 1)
                if m % 16 == 15:
                    dve.wait_ge(maxed, UNITS * j + m + 1)
                    dve.tensor_reduce(mxw[p][:, DK:KB], mxp[p][:, :, :], AX_X, ALU.max).then_inc(mx_ready, 1)

            def place_max(j, par, p):
                dve.wait_ge(c_done, 2 * j + p + 1)
                rows = ps_x[p][DK:KB, 0:P].rearrange("r (o q) -> r o q", o=1).to_broadcast([NB, QT, P])
                dve.tensor_tensor(qB[par][p][DK:KB, :].rearrange("r (t q) -> r t q", q=P), rows,
                                  rowmask[DK:KB, :].rearrange("r (t q) -> r t q", q=P), ALU.mult).then_inc(c_placed, 1)

            def recip(j, half, quarter):
                c = half * HALF + quarter * P
                if quarter == 0:
                    dve.wait_ge(sums_done, 2 * j + half + 1)
                dve.reciprocal(rc[:, c:c + P], ps_x[half][:, quarter * P:(quarter + 1) * P]).then_inc(recip_done, 1)
                if quarter == 3:
                    dve.wait_ge(recip_done, 8 * j + 4 * half + 4)
                    dve.wait_ge(z_copied, 2 * j + half + 1)
                    d = slice(half * HALF, (half + 1) * HALF)
                    dve.tensor_tensor(zT[:, d], zr[:, d], rc[:, d], ALU.mult).then_inc(z_ready, 1)

            def add_wo(j, g):
                dve.wait_ge(wo_done, 2 * j + g + 1)
                at = x2[:, bass.ds((j // HP) * S + g * HALF, HALF)]
                dve.tensor_tensor(at, ps_x[g][:, :], at, ALU.add).then_inc(wo_added, 1)

            def pair(j, par, first=False, second=False, last=False, routes=None):
                for u in range(UNITS + 1):
                    if first or second:
                        if u == STATS_AT:
                            first_moments(2 + j)
                        if u == NORM_AT:
                            first_norm(2 + j)
                    if second and u == UNITS:
                        clear_rows()
                    if routes is not None:
                        if u == STATS_AT:
                            second_moments(routes)
                        if u == NORM_AT:
                            second_norm(routes)
                        if u - 1 == LOGITS_AT:
                            choose(routes)
                        if u - 1 == RANKS_AT:
                            find_slots(routes)
                    if not last and u - 1 in C_AT:
                        place_max(j + 1, 1 - par, C_AT[u - 1])
                    if not last:
                        for m in max_units(u):
                            reduce_max(j + 1, m)
                        if u - LOW_Q in QK_AT:
                            low_qk(j + 1, 1 - par, QK_AT[u - LOW_Q], True)
                        if u - LOW_K in QK_AT:
                            low_qk(j + 1, 1 - par, QK_AT[u - LOW_K], False)
                    if not (first or second) and u - 1 in WO_AT:
                        add_wo(j - 2, WO_AT[u - 1])
                    if not first and u in RECIP_AT:
                        recip(j - 1, *RECIP_AT[u])

            for use in range(4):
                low_qk(0, 0, use, True)
                low_qk(0, 0, use, False)
            for m in range(UNITS):
                reduce_max(0, m)
            for p in range(2):
                place_max(0, 0, p)
            pair(0, 0, first=True)
            pair(1, 1, second=True)
            with dve.Fori(0, PAIR_LOOP) as i:
                for par in range(2):
                    pair(2 * i + 2 + par, par)
            for b in range(B - 1):
                pair(ROUTE_FROM + b, b % 2, routes=b)
            pair(PAIRS - 1, 1, last=True)
            for g in range(2):
                add_wo(PAIRS - 2, g)
            for n in range(8):
                recip(PAIRS - 1, *divmod(n, 4))
            for g in range(2):
                add_wo(PAIRS - 1, g)

            second_moments(B - 1)
            second_norm(B - 1)
            choose(B - 1)
            find_slots(B - 1)

            def finish(e):
                dve.wait_ge(down_done, e + 1)
                if e >= 2:
                    dve.wait_ge(stored[e % 2], 16 * ST * (e // 2))
                for n in range(ST):
                    dve.scalar_tensor_tensor(out=ye[e % 2][:, n * D:(n + 1) * D], in0=ps_z[e % 2][:, n * D:(n + 1) * D],
                                             scalar=xe(e)[:, n, 2 * D:2 * D + 1], in1=xe(e)[:, n, D:2 * D],
                                             op0=ALU.mult, op1=ALU.add).then_inc(ye_ready, 1)

            for e in range(E):
                if e >= 2:
                    dve.wait_ge(down_done, e - 1)
                for c in range(FC):
                    n = e * FC + c
                    dve.wait_ge(up_done, n + 1)
                    dve.tensor_scalar(rT[e % 2][:, c * HALF:(c + 1) * HALF], ps_s[n % 2][:, :], 0.0, None,
                                      ALU.max).then_inc(relu_done, 1)
                if e >= 1:
                    finish(e - 1)
            finish(E - 1)

        @block.tensor
        def _(pe):
            pe.wait_ge(consts, 4)
            pe.wait_ge(dve_consts, 13)
            def turn_h(b, g):
                pe.wait_ge(h_ready, b + 1)
                for i in range(4):
                    mm = pe.transpose(ps_x[g][:, i * P:(i + 1) * P], h_tok(b)[:, 4 * g + i, :], ident[:, :])
                mm.then_inc(h_turned, 1)

            def turned(j, par):
                return hT if isinstance(j, int) and j == 0 else hTs[par]

            def project_qk(j, par, use):
                p, half = divmod(use, 2)
                if use == 0:
                    pe.wait_ge(w_loaded[par], 64 * (j // 2) + (64 if par else 48))
                pe.matmul(ps_x[use % 2][:, :], wst[par][:, p * P:(p + 1) * P],
                          turned(j, par)[:, half * HALF:(half + 1) * HALF], start=True, stop=True).then_inc(qk_done, 1)

            def project_v(j, par, half):
                pe.wait_ge(qk_low, 4 * j + 2 + half + 1)
                for i in range(4):
                    t = 4 * half + i
                    mm = pe.matmul(ps_x[half][:, i * P:(i + 1) * P], turned(j, par)[:, t * P:(t + 1) * P],
                                   wst[par][:, 4 * DK:6 * DK], start=True, stop=True)
                mm.then_inc(v_done, 1)

            def max_scores(j, par, m):
                p, qt, kh = m // 16, (m // 2) % 8, m % 2
                if m % 16 == 0:
                    pe.wait_ge(qk_low, 4 * j + 2 * p + 2)
                    pe.wait_ge(qk_cast_again, 4 * j + 2 * p + 2)
                if not (isinstance(j, int) and j == 0 and m < 2):
                    pe.wait_ge(maxed, UNITS * j + m - 1)
                pe.matmul(ps_m[m % 2][:, :], qA[par][p][:, qt * P:(qt + 1) * P],
                          kA[par][p][:, kh * HALF:(kh + 1) * HALF], start=True, stop=True).then_inc(m_done, 1)

            def turn_max(j, p):
                pe.wait_ge(mx_ready, 2 * j + p + 1)
                pe.transpose(ps_x[p][0:KB, 0:P], mxw[p][:, :], ident[:, :]).then_inc(c_done, 1)

            def scores(j, par, u):
                kt, half, p = u // 4, (u // 2) % 2, u % 2
                if u < 2:
                    pe.wait_ge(c_placed, 2 * j + u + 1)
                if not (isinstance(j, int) and j == 0 and u < 2):
                    pe.wait_ge(exp_done, UNITS * j + u - 1)
                c = slice(half * HALF, (half + 1) * HALF)
                k = slice(kt * P, (kt + 1) * P)
                pe.matmul(ps_s[u % 2][:, :], kA[par][p][:, k], qA[par][p][:, c], start=True, stop=False)
                pe.matmul(ps_s[u % 2][:, :], kB[par][p][:, k], qB[par][p][:, c], start=False,
                          stop=True).then_inc(scores_ready, 1)

            def values(j, par, kt, half, first=False):
                if kt == 0:
                    pe.wait_ge(v_copied, 2 * j + 2)
                    if not first:
                        pe.wait_ge(z_copied, 2 * j - 1 + half)
                for p in range(2):
                    mm = pe.matmul(ps_z[half][p * DK:(p + 1) * DK, :],
                                   V[par][:, kt * P + p * DK:kt * P + (p + 1) * DK], P_tile(kt, p, half),
                                   start=(kt == 0), stop=(kt == KT - 1))
                mm.then_inc(pv_done, 1)

            def softmax_sums(j, par, half, by_pe=0):
                pe.wait_ge(summed, 14 * j + 14 - 2 * by_pe)
                for p in range(2):
                    at = p * S + half * HALF
                    parts = [acc[par][:, at:at + HALF]] + [P_tile(kt, p, half) for kt in range(KT - by_pe, KT)]
                    for i, part in enumerate(parts):
                        mm = pe.matmul(ps_x[half][p * DK:(p + 1) * DK, :], ones[:, :], part,
                                       start=(i == 0), stop=(i == len(parts) - 1))
                mm.then_inc(sums_done, 1)

            def project_out(j, par, g):
                pe.wait_ge(wo_loaded[par], 16 * (j // 2) + 16)
                pe.wait_ge(z_ready, 2 * j + g + 1)
                for i in range(4):
                    t = 4 * g + i
                    mm = pe.matmul(ps_x[g][:, i * P:(i + 1) * P], zT[:, t * P:(t + 1) * P], wo[par][:, :],
                                   start=True, stop=True)
                mm.then_inc(wo_done, 1)

            def turn_h2(b, g):
                pe.wait_ge(h2_ready, b + 1)
                for i in range(4):
                    mm = pe.transpose(ps_x[g][:, i * P:(i + 1) * P], rows[:, 4 * g + i, 0:D], ident[:, :])
                mm.then_inc(h2_turned, 1)

            def make_logits(b):
                pe.wait_ge(wr_loaded, 16)
                pe.wait_ge(h2T_ready, 2 * b + 2)
                for t in range(QT):
                    mm = pe.matmul(ps_x[0][:, t * E:(t + 1) * E], h2T[:, t * P:(t + 1) * P], wr[:, :],
                                   start=True, stop=True)
                mm.then_inc(logits_done, 1)

            def count_ranks(b):
                pe.wait_ge(onehot_ready, b + 1)
                made = ps_x[1][:, 0:(QT + 1) * E].rearrange("p (t e) -> p t e", e=E)
                pe.matmul(ps_x[1][:, 0:(QT + 1) * E], upper[:, :], hot_b[:, b, :], start=True, stop=False,
                          skip_group_check=True)
                for t in range(QT):
                    one = hot_b[:, b, t * E:(t + 1) * E].rearrange("p (o e) -> p o e", o=1)
                    mm = pe.matmul(made[:, t + 1:QT + 1, :], ones_b[:, :], one.to_broadcast([P, QT - t, E]),
                                   start=False, stop=(t == QT - 1), skip_group_check=True)
                mm.then_inc(ranks_done, 1)

            def pair(j, par, first=False, second=False, last=False, routes=None):
                nxt = 1 - par
                for u in range(UNITS):
                    kt, odd = u // 4, u % 4
                    scores(j, par, u)
                    ms = list(max_units(u)) if not last else []
                    for m in ms[:1]:
                        max_scores(j + 1, nxt, m)
                    if odd in (1, 3) and (kt > 0 or not first):
                        half = odd // 2
                        if kt > 0:
                            values(j, par, kt - 1, half, first)
                        else:
                            values(j - 1, nxt, KT - 1, half, second)
                    if not last and u in QK_AT:
                        use = QK_AT[u]
                        if use >= 2:
                            pe.wait_ge(qk_low, 4 * (j + 1) + use - 1)
                        elif first or second:
                            pe.wait_ge(c_placed, 2 * j + use + 1)
                        else:
                            pe.wait_ge(recip_done, 8 * (j - 2) + 4 * use + 4)
                        project_qk(j + 1, nxt, use)
                    if not last and u in V_AT:
                        project_v(j + 1, nxt, V_AT[u])
                    if (first or second) and u in EARLY_TURN_AT[j]:
                        b, g = EARLY_TURN_AT[j][u]
                        if u < min(C_AT):
                            pe.wait_ge(v_copied, 2 * (j + 1) + g + 1)
                        elif g == 0:
                            pe.wait_ge(c_placed, 2 * (j + 1) + 1)
                        else:
                            pe.wait_ge(hT_ready, 2 * b)
                        turn_h(b, g)
                    if routes is not None and u in TURN_AT:
                        pe.wait_ge(v_copied, 2 * (j + 1) + TURN_AT[u] + 1)
                        turn_h2(routes, TURN_AT[u])
                    if not (first or second) and u in WO_AT:
                        if last:
                            pe.wait_ge(recip_done, 8 * (j - 2) + 4 * WO_AT[u] + 4)
                        elif routes is not None:
                            pe.wait_ge(h2T_ready, 2 * routes + WO_AT[u] + 1)
                        else:
                            pe.wait_ge(v_copied, 2 * (j + 1) + WO_AT[u] + 1)
                        project_out(j - 2, par, WO_AT[u])
                    if not last and u in C_AT:
                        p = C_AT[u]
                        if first or second:
                            pe.wait_ge(hT_ready, max(2 * b + g + 1 for v, (b, g) in EARLY_TURN_AT[j].items()
                                                     if v < u and g == p))
                        elif routes is not None and p == 1:
                            pe.wait_ge(index_ready, routes + 1)
                        else:
                            pe.wait_ge(wo_added, 2 * (j - 2) + p + 1)
                        turn_max(j + 1, p)
                    if routes is not None and u == LOGITS_AT:
                        pe.wait_ge(c_placed, 2 * (j + 1) + 1)
                        make_logits(routes)
                    if routes is not None and u == RANKS_AT:
                        pe.wait_ge(wo_added, 2 * (j - 2) + 2)
                        count_ranks(routes)
                    if not first and u in SUM_AT:
                        half = SUM_AT[u]
                        if last:
                            pe.wait_ge(wo_added, 2 * (j - 2) + half + 1)
                        elif routes is not None and half == 0:
                            pe.wait_ge(onehot_ready, routes + 1)
                        else:
                            pe.wait_ge(c_placed, 2 * (j + 1) + half + 1)
                        softmax_sums(j - 1, nxt, half)
                    for m in ms[1:]:
                        max_scores(j + 1, nxt, m)

            for g in range(2):
                turn_h(0, g)
            for use in range(4):
                if use < 2:
                    pe.wait_ge(hT_ready, 2)
                else:
                    pe.wait_ge(qk_low, use - 1)
                project_qk(0, 0, use)
            for half in range(2):
                project_v(0, 0, half)
            for m in range(UNITS):
                max_scores(0, 0, m)
            for p in range(2):
                pe.wait_ge(v_copied, p + 1)
                turn_max(0, p)
            pair(0, 0, first=True)
            pair(1, 1, second=True)
            with pe.Fori(0, PAIR_LOOP) as i:
                for par in range(2):
                    pair(2 * i + 2 + par, par)
            for b in range(B - 1):
                pair(ROUTE_FROM + b, b % 2, routes=b)
            last = PAIRS - 1
            pair(last, 1, last=True)
            pe.wait_ge(exp_done, UNITS * PAIRS)
            for half in range(2):
                values(last, 1, KT - 1, half)
            for g in range(2):
                pe.wait_ge(recip_done, 8 * (last - 1) + 4 * g + 4)
                project_out(last - 1, 0, g)
            for half in range(2):
                pe.wait_ge(wo_added, 2 * (last - 1) + half + 1)
                softmax_sums(last, 1, half, LAST_BY_PE)
            for g in range(2):
                project_out(last, 1, g)

            pe.wait_ge(wo_added, 2 * PAIRS)
            for g in range(2):
                turn_h2(B - 1, g)
            make_logits(B - 1)
            count_ranks(B - 1)

            def turn_tokens(e):
                pe.wait_ge(xe_loaded[e % XE], 16 * (e // XE + 1))
                if e >= 2:
                    pe.wait_ge(xeT_ready, e - 1)
                for i in range(ST):
                    mm = pe.transpose(ps_x[e % 2][:, i * P:(i + 1) * P], xe(e)[:, i, 0:D], ident[:, :])
                mm.then_inc(xe_turned, 1)

            def down(e):
                if e >= 2:
                    pe.wait_ge(ye_ready, ST * (e - 1))
                pe.wait_ge(relu_done, FC * (e + 1))
                for st in range(ST):
                    for c in range(FC):
                        mm = pe.matmul(ps_z[e % 2][:, st * P:(st + 1) * P],
                                       rT[e % 2][:, c * HALF + st * P:c * HALF + (st + 1) * P],
                                       w2_sb[:, (c * E + e) * D:(c * E + e + 1) * D], start=(c == 0), stop=(c == FC - 1))
                mm.then_inc(down_done, 1)

            pe.wait_ge(w1_loaded, 16)
            pe.wait_ge(w2_loaded, 16 * FC)
            turn_tokens(0)
            for e in range(E):
                if e + 1 < E:
                    turn_tokens(e + 1)
                pe.wait_ge(xeT_ready, e + 1)
                for c in range(FC):
                    n = e * FC + c
                    if n >= 2:
                        pe.wait_ge(relu_done, n - 1)
                    pe.matmul(ps_s[n % 2][:, :], w1_sb[:, e * F + c * P:e * F + (c + 1) * P],
                              xeT[e % 2][:, :], start=True, stop=True).then_inc(up_done, 1)
                if e >= 1:
                    down(e - 1)
            down(E - 1)


_INS = ["L0_attn_x", "L0_attn_w_q", "L0_attn_w_k", "L0_attn_w_v", "L0_attn_w_o", "L0_ffn_Wr", "L0_ffn_W1", "L0_ffn_W2"]


def kernel(**inputs):
    import numpy as _np
    import concourse.bacc as _bacc
    from concourse import mybir as _mybir
    from concourse.bass_utils import run_bass_kernel_spmd as _run

    nc = _bacc.Bacc("TRN2", target_bir_lowering=False, num_devices=1)
    arrays, args = {}, []
    for name in _INS:
        a = _np.ascontiguousarray(inputs[name])
        arrays[f"in_{name}"] = a
        args.append(nc.dram_tensor(f"in_{name}", a.shape, _mybir.dt.from_np(a.dtype), kind="ExternalInput").ap())
    shape = inputs["L0_attn_x"].shape
    args.append(nc.dram_tensor("out_0", shape, _mybir.dt.float32, kind="ExternalOutput").ap())
    block_kernel(nc, *args)
    r = _run(nc, [arrays], core_ids=[0])
    return r.results[0]["out_0"]
```

```python
from contextlib import ExitStack

import concourse.bass as bass
from concourse import mybir

F32 = mybir.dt.float32
F32R = mybir.dt.float32r
I32 = mybir.dt.int32
U32 = mybir.dt.uint32
BF16 = mybir.dt.bfloat16
ALU = mybir.AluOpType
ACT = mybir.ActivationFunctionType
AX_X = mybir.AxisListType.X

P = 128
HALF = 512
EPS = 1e-5

QK_AT = {0: 0, 1: 1, 4: 2, 6: 3}
V_AT = {8: 0, 9: 1}
C_AT = {17: 0, 25: 1}
SUM_AT = {24: 0, 27: 1}
RECIP_AT = {25: (0, 0), 26: (0, 1), 27: (0, 2), 28: (0, 3), 29: (1, 0), 30: (1, 1), 31: (1, 2), 32: (1, 3)}
WO_AT = {14: 0, 21: 1}
MAX_FROM, MAX_TO = 4, 25
UNITS = 32
LOW_Q, LOW_K = 2, 2
Z_AT = {2: 0, 4: 1}

STATS_AT = 1
NORM_AT = 10
TURN_AT = {11: 0, 12: 1}
SUM_COPY_AT = {15: 0, 16: 1}
LOGITS_AT = 20
SHARE_AT = 22
RANKS_AT = 23

EARLY_TURN_AT = [{11: (1, 0), 12: (1, 1), 20: (2, 0), 21: (2, 1)}, {11: (3, 0), 12: (3, 1)}]
SPLIT_AT = {13: 0, 15: 1, 19: 2}
LOW_BEFORE = 5
PLACE_BEFORE = {4: 0, 6: 1}
RESIDUAL_AFTER = 4


def max_units(u):
    def before(v):
        return UNITS * min(max(v - MAX_FROM, 0), MAX_TO - MAX_FROM) // (MAX_TO - MAX_FROM)
    return range(before(u), before(u + 1))


def block_kernel(nc, x_in, w_q, w_k, w_v, w_o, w_r, w_1, w_2, out):
    B, S, D = x_in.shape
    H, _, DK = w_q.shape
    E, _, F = w_1.shape
    T = B * S
    TT = T // P
    QT = S // P
    KT = S // P
    PAIRS = B * H // 2
    HP = H // 2
    CAP = -(-T // E)
    FC = F // P
    ST = CAP // P
    SCALE = 1.0 / float(DK) ** 0.5
    NB = 8
    KB = DK + NB
    RING = 4
    assert D == P and 2 * DK == P and 2 * HALF == S and QT == NB and CAP == HALF and PAIRS % 2 == 0
    assert UNITS == 4 * KT

    x_t = x_in.rearrange("b (n p) d -> b p n d", p=P)
    out_t = out.rearrange("b (n p) d -> b p n d", p=P)
    wq_d = w_q.rearrange("h d k -> d h k")
    wk_d = w_k.rearrange("h d k -> d h k")
    wv_d = w_v.rearrange("h d k -> d h k")
    wo_d = w_o.rearrange("(h p) d -> p h d", p=P)
    W = 2 * D + 2
    slots_d = nc.dram_tensor("tokens_by_slot", (E * CAP, W), F32, kind="Internal").ap()
    out_rows = out.rearrange("b s d -> (b s) d")

    with ExitStack() as ctx:
        def sb(name, shape, dt=F32):
            return ctx.enter_context(nc.sbuf_tensor(name, shape, dt))

        def sem(name):
            return ctx.enter_context(nc.semaphore(name))

        x2 = sb("x2", [P, TT * D])
        ring = sb("ring", [P, RING * 2 * S])
        ident = sb("ident", [P, P])
        upper = sb("upper", [P, P], BF16)
        ones_b = sb("ones_b", [P, P], BF16)
        moments = sb("moments", [P, 2 * B, QT, 2])
        moment_parts = sb("moment_parts", [P, QT, 6])
        roots = sb("roots", [P, 2 * B, 3, QT])
        rows = sb("rows", [P, QT, W])
        wr = sb("wr", [P, E])
        lg, ex, hot = (sb(n, [P, TT * E])[:, :].rearrange("p (t e) -> p t e", e=E)
                             for n in ("logits", "shifted_logits", "one_hot"))
        iota_e = sb("expert_no", [P, QT * E])[:, :].rearrange("p (t e) -> p t e", e=E)
        hot_b = sb("one_hot_b", [P, B, (QT + 1) * E], BF16)
        seen = sb("seen", [P, B + 1, E])
        cols = sb("routing_columns", [P, 6, TT])
        scatter_at = sb("scatter_at", [P, TT], I32)

        with ExitStack() as later:
            def sb_later(name, shape, dt=F32):
                return later.enter_context(nc.sbuf_tensor(name, shape, dt))

            w1_sb = sb_later("w1", [P, E * F])
            w2_sb = sb_later("w2", [P, FC * E * D])
            w1_high, w1_low = (sb_later(n, [P, E * F], F32R) for n in ("w1_high", "w1_low"))
            xeT_high, xeT_low = ([sb_later(f"{n}{i}", [P, HALF], F32R) for i in range(2)]
                                 for n in ("xeT_high", "xeT_low"))
            rT = [sb_later(f"rT{i}", [P, FC * HALF]) for i in range(2)]
            ye = [sb_later(f"ye{i}", [P, HALF]) for i in range(2)]

        kA = [[sb(f"kA{i}{p}", [P, S], F32R) for p in range(2)] for i in range(2)]
        qA = [[sb(f"qA{i}{p}", [P, S], F32R) for p in range(2)] for i in range(2)]
        kB = [[sb(f"kB{i}{p}", [KB, S], F32R) for p in range(2)] for i in range(2)]
        qB = [[sb(f"qB{i}{p}", [KB, S], F32R) for p in range(2)] for i in range(2)]
        hT = sb("hT", [P, T])
        h2T = hT[:, 0:S]
        hTs = [sb(f"hTs{i}", [P, S]) for i in range(2)]
        wst = [sb(f"wst{i}", [P, 6 * DK]) for i in range(2)]
        wo = [sb(f"wo{i}", [P, D]) for i in range(2)]
        h_high, h_low = (sb(n, [P, S], F32R) for n in ("h_high", "h_low"))
        w_high, w_low = (sb(n, [P, 4 * DK], F32R) for n in ("w_high", "w_low"))
        V = [sb(f"V{i}", [P, KT * P]) for i in range(2)]
        acc = [sb(f"acc{i}", [P, 2 * S]) for i in range(2)]
        zr = sb("zr", [P, S])
        zT = sb("zT", [P, S])
        rc = sb("rc", [P, S])
        mxp = [sb(f"mxp{p}", [P, QT, 2]) for p in range(2)]
        mxw = [sb(f"mxw{p}", [P, KB]) for p in range(2)]
        mxr = [sb(f"mxr{p}", [KB, P]) for p in range(2)]
        rowmask = sb("rowmask", [KB, S])
        ones = sb("ones", [P, DK])

        XE = min(E, RING * 2 * S // (ST * W))
        def xe(e):
            at = (e % XE) * ST * W
            return ring[:, at:at + ST * W].rearrange("p (n w) -> p n w", w=W)

        def P_tile(kt, p, half):
            at = ((kt % RING) * 2 + p) * S + half * HALF
            return ring[:, at:at + HALF]

        ps_s = [ctx.enter_context(nc.psum_tensor(f"ps_s{i}", [P, HALF], F32)) for i in range(2)]
        ps_m = [ctx.enter_context(nc.psum_tensor(f"ps_m{i}", [P, HALF], F32)) for i in range(2)]
        ps_z = [ctx.enter_context(nc.psum_tensor(f"ps_z{i}", [P, HALF], F32)) for i in range(2)]
        ps_x = [ctx.enter_context(nc.psum_tensor(f"ps_x{i}", [P, HALF], F32)) for i in range(2)]

        x_loaded = [sem(f"x_loaded{b}") for b in range(B)]
        w_loaded = [sem(f"w_loaded{i}") for i in range(2)]
        wo_loaded = [sem(f"wo_loaded{i}") for i in range(2)]
        wr_loaded = sem("wr_loaded")
        consts = sem("consts")
        dve_consts = sem("dve_consts")
        chain = sem("chain")
        moments_ready = sem("moments_ready")
        root_ready = sem("root_ready")
        root_chain = sem("root_chain")
        h_ready = sem("h_ready")
        residual_ready = sem("residual_ready")
        h_turned = sem("h_turned")
        hT_ready = sem("hT_ready")

        high_split = sem("high_split")
        low_split = sem("low_split")
        qk_done = sem("qk_done")
        qk_cast = sem("qk_cast")
        q_again = sem("q_again")
        k_copied = sem("k_copied")
        qk_copied = sem("qk_copied")
        qk_low = sem("qk_low")
        v_done = sem("v_done")
        v_copied = sem("v_copied")
        m_done = sem("m_done")
        maxed = sem("maxed")
        mx_ready = sem("mx_ready")
        c_done = sem("c_done")
        c_copied = sem("c_copied")
        c_placed = sem("c_placed")
        scores_ready = sem("scores_ready")
        exp_done = sem("exp_done")
        pv_done = sem("pv_done")
        summed = sem("summed")
        sums_done = sem("sums_done")
        z_copied = sem("z_copied")
        recip_done = sem("recip_done")
        z_ready = sem("z_ready")
        wo_done = sem("wo_done")
        wo_added = sem("wo_added")

        rows_cleared = sem("rows_cleared")
        row_numbers = sem("row_numbers")
        slots_cleared = sem("slots_cleared")
        w1_loaded = sem("w1_loaded")
        w2_loaded = sem("w2_loaded")
        h2_ready = sem("h2_ready")
        sum_copied = sem("sum_copied")
        h2_turned = sem("h2_turned")
        h2T_ready = sem("h2T_ready")
        logits_done = sem("logits_done")
        shifted = sem("shifted")
        route_exp = sem("route_exp")
        onehot_ready = sem("onehot_ready")
        ranks_done = sem("ranks_done")
        index_ready = sem("index_ready")
        scattered = [sem(f"scattered{b}") for b in range(B)]
        residual_stored = sem("residual_stored")
        xe_loaded = [sem(f"xe_loaded{i}") for i in range(XE)]
        xe_turned = sem("xe_turned")
        w1_split = sem("w1_split")
        w1_ready = sem("w1_ready")
        xeT_split = sem("xeT_split")
        xeT_ready = sem("xeT_ready")
        up_done = sem("up_done")
        relu_done = [sem(f"relu_done{i}") for i in range(2)]
        down_done = sem("down_done")
        ye_ready = sem("ye_ready")
        stored = [sem(f"stored{i}") for i in range(2)]

        def h_tok(b):
            return rows[:, :, (b % 2) * D:(b % 2 + 1) * D]

        block = ctx.enter_context(nc.Block())

        PAIR_LOOP = (PAIRS - 6) // 2
        LAST_BY_PE = 2
        ROUTE_FROM = PAIRS - 4
        assert 8 * (B - 1) + 2 <= ROUTE_FROM + B - 2 and PAIRS - 1 - ROUTE_FROM == B - 1

        @block.sync
        def _(sp):
            for b in range(B):
                sp.dma_start(x2[:, b * S:(b + 1) * S].rearrange("p (n d) -> p n d", d=D),
                             x_t[b]).then_inc(x_loaded[b], 16)
            sp.dma_start(wr[:, :], w_r).then_inc(wr_loaded, 16)

            def load_weights(j, par):
                hp, b = j % HP, j // HP
                view = wst[par][:, 0:4 * DK].rearrange("p (h t k) -> p h t k", h=2, t=2)
                sp.dma_start(view[:, :, 0, :], wq_d[:, bass.ds(2 * hp, 2), :]).then_inc(w_loaded[par], 16)
                sp.dma_start(view[:, :, 1, :], wk_d[:, bass.ds(2 * hp, 2), :]).then_inc(w_loaded[par], 16)
                sp.dma_start(wst[par][:, 4 * DK:6 * DK].rearrange("p (h k) -> p h k", h=2),
                             wv_d[:, bass.ds(2 * hp, 2), :]).then_inc(w_loaded[par], 16)
                if not (isinstance(j, int) and j == 0):
                    sp.wait_ge(hT_ready, 2 * b + 2)
                    sp.dma_start(hTs[par][:, :], hT[:, bass.ds(b * S, S)]).then_inc(w_loaded[par], 16)

            def load_wo(j, par):
                sp.dma_start(wo[par][:, :].rearrange("p (o d) -> p o d", o=1),
                             wo_d[:, bass.ds(j % HP, 1), :]).then_inc(wo_loaded[par], 16)

            for j in range(2):
                load_weights(j, j)
                load_wo(j, j)

            def copy_high(j, par):
                for use in range(4):
                    p, half = divmod(use, 2)
                    c = slice(half * HALF, (half + 1) * HALF)
                    sp.wait_ge(qk_cast, 4 * j + use + 1)
                    done = qk_copied if p else k_copied
                    if p == 1:
                        sp.dma_start(qA[par][p][DK:P, c].bitcast(F32),
                                     qA[par][p][0:DK, c].bitcast(F32)).then_inc(done, 16)
                    sp.dma_start(kB[par][p][0:DK, c].bitcast(F32),
                                 kA[par][p][DK:P, c].bitcast(F32)).then_inc(done, 16)

            def transfers(j, par):
                copy_high(j, par)
                if not (isinstance(j, int) and j == PAIRS - 1):
                    sp.wait_ge(v_done, 2 * j)
                    load_weights(j + 1, 1 - par)
                if not (isinstance(j, int) and j < 3):
                    sp.wait_ge(wo_done, 2 * j - 4)
                    load_wo(j - 1, 1 - par)

            copy_high(0, 0)
            for j in range(1, 3):
                transfers(j, j % 2)

            sp.wait_ge(rows_cleared, 2)
            for n in range(E * CAP // S):
                sp.dma_start(slots_d[n * S:(n + 1) * S, :].rearrange("(p n) w -> p n w", p=P),
                             rows[:, :, :]).then_inc(slots_cleared, 16)
            with sp.Fori(0, PAIR_LOOP - 1) as i:
                for q in range(2):
                    transfers(2 * i + 3 + q, 1 - q)
            for j in range(2 * PAIR_LOOP + 1, PAIRS):
                transfers(j, j % 2)
            sp.wait_ge(wo_done, 2 * PAIRS - 4)
            load_wo(PAIRS - 1, (PAIRS - 1) % 2)

            sp.wait_ge(scores_ready, UNITS * PAIRS)
            sp.dma_start(w1_sb[:, :].rearrange("p (e f) -> p e f", e=E),
                         w_1.rearrange("e d f -> d e f")).then_inc(w1_loaded, 16)
            for c in range(FC):
                sp.dma_start(w2_sb[:, c * E * D:(c + 1) * E * D].rearrange("p (e d) -> p e d", e=E),
                             w_2.rearrange("e (c p) d -> c p e d", p=P)[c]).then_inc(w2_loaded, 16)

            for b in range(B):
                sp.wait_ge(wo_added, 2 * HP * (b + 1))
                sp.dma_start(out_t[b], x2[:, b * S:(b + 1) * S].rearrange("p (n d) -> p n d", d=D)
                             ).then_inc(residual_stored, 16)

            for b in range(B):
                sp.wait_ge(scattered[b], 16 * QT)
            for e in range(E):
                if e >= XE:
                    sp.wait_ge(stored[(e - XE) % 2], 16 * ST * ((e - XE) // 2 + 1))
                sp.dma_start(xe(e), slots_d[e * CAP:(e + 1) * CAP, :].rearrange("(n p) w -> p n w", p=P)
                             ).then_inc(xe_loaded[e % XE], 16)
            for i in range(2):
                sp.wait_ge(stored[i], 16 * ST * E // 2)

        @block.gpsimd
        def _(pool):
            pool.wait_ge(dve_consts, 3)
            pool.affine_select(out=ident[:, :], in_=ident[:, :], compare_op=ALU.is_equal, fill=0.0,
                               base=0, pattern=[[-1, P]], channel_multiplier=1).then_inc(consts, 1)
            pool.affine_select(out=rowmask[:, :].rearrange("p (t q) -> p t q", q=P),
                               in_=rowmask[:, :].rearrange("p (t q) -> p t q", q=P),
                               compare_op=ALU.is_equal, fill=0.0, base=-DK,
                               pattern=[[-1, NB], [0, P]], channel_multiplier=1).then_inc(consts, 1)
            pool.affine_select(out=upper[:, :], in_=upper[:, :], compare_op=ALU.is_gt, fill=0.0,
                               base=0, pattern=[[1, P]], channel_multiplier=-1).then_inc(consts, 1)
            pool.iota(iota_e, pattern=[[0, QT], [1, E]], base=0, channel_multiplier=0,
                      allow_small_or_imprecise_dtypes=True).then_inc(consts, 1)

            steps = [0]

            def then(ins):
                steps[0] += 1
                ins.then_inc(root_chain, 1)
                pool.wait_ge(root_chain, steps[0])

            def inverse_root(n):
                v, y, t = (roots[:, n, k, :] for k in range(3))
                pool.wait_ge(moments_ready, n + 1)
                then(pool.tensor_scalar(v, moments[:, n, :, 1], EPS, None, ALU.add))
                then(pool.tensor_scalar(y.bitcast(I32), v.bitcast(I32), -0.5, float(0x5F3759DF), ALU.mult, ALU.add))
                for step in range(3):
                    then(pool.tensor_tensor(t, y, y, ALU.mult))
                    then(pool.tensor_tensor(t, t, v, ALU.mult))
                    then(pool.tensor_scalar(t, t, -0.5, 1.5, ALU.mult, ALU.add))
                    if step < 2:
                        then(pool.tensor_tensor(y, y, t, ALU.mult))
                pool.tensor_tensor(y, y, t, ALU.mult).then_inc(root_ready, 1)

            def residual(b):
                pool.wait_ge(h_ready, b + 1)
                at = x2[:, b * S:(b + 1) * S].rearrange("p (t d) -> p t d", d=D)
                pool.tensor_tensor(at, at, h_tok(b), ALU.add).then_inc(residual_ready, 1)

            for b in range(2):
                inverse_root(b)
            for b in range(2):
                residual(b)

            def number_rows(b):
                if b == 0:
                    pool.wait_ge(slots_cleared, 16 * (E * CAP // S))
                else:
                    pool.wait_ge(scattered[b - 1], 16 * QT)
                pool.iota(rows[:, :, W - 1].bitcast(I32), pattern=[[P, QT]], base=b * S,
                          channel_multiplier=1).then_inc(row_numbers, 1)

            def scatter(b):
                pool.wait_ge(row_numbers, b + 1)
                pool.wait_ge(index_ready, b + 1)
                pool.wait_ge(sum_copied, 2 * b + 2)
                for t in range(QT):
                    i = b * QT + t
                    pool.indirect_dma_start(
                        out=slots_d, in_=rows[:, t, :], in_offset=None,
                        out_offset=bass.IndirectOffsetOnAxis(ap=scatter_at[:, i:i + 1].bitcast(U32), axis=0),
                        bounds_check=E * CAP - 1, oob_is_err=False).then_inc(scattered[b], 16)

            def place_max(j, par, p):
                pool.wait_ge(c_copied, 2 * j + p + 1)
                spread = mxr[p][DK:KB, :].rearrange("r (o q) -> r o q", o=1).to_broadcast([NB, QT, P])
                pool.tensor_tensor(qB[par][p][DK:KB, :].rearrange("r (t q) -> r t q", q=P), spread,
                                   rowmask[DK:KB, :].rearrange("r (t q) -> r t q", q=P), ALU.mult).then_inc(c_placed, 1)
                pool.wait_ge(c_placed, 2 * j + p + 1)

            def split_low(j, par):
                pool.wait_ge(high_split, 3 * (j - 2) + 3)
                pool.tensor_tensor(h_low[:, :], hTs[par][:, :], h_high[:, :].bitcast(F32),
                                   ALU.subtract).then_inc(low_split, 1)
                pool.tensor_tensor(w_low[:, :], wst[par][:, 0:4 * DK], w_high[:, :].bitcast(F32),
                                   ALU.subtract).then_inc(low_split, 1)

            def add_up(j, par, early=None, routes=None, upto=KT, last=False):
                if routes is not None:
                    inverse_root(B + routes)
                    number_rows(routes)
                if early is not None:
                    inverse_root(early)
                for kt in range(1, upto):
                    if kt == LOW_BEFORE and not (last or routes == B - 2):
                        split_low(j + 2, par)
                    if not last and kt in PLACE_BEFORE:
                        pool.wait_ge(summed, 14 * j + 2 * (kt - 1))
                        place_max(j + 1, 1 - par, PLACE_BEFORE[kt])
                    if early is not None and kt == RESIDUAL_AFTER + 1:
                        residual(early)
                    if routes is not None and kt == KT - 1:
                        scatter(routes)
                    for p in range(2):
                        a = acc[par][:, p * S:(p + 1) * S]
                        n = 2 * (kt - 1) + p
                        pool.wait_ge(exp_done, UNITS * j + 4 * kt + 3 + p)
                        if kt > 1:
                            pool.wait_ge(summed, 14 * j + n - 1)
                        before = a if kt > 1 else ring[:, p * S:(p + 1) * S]
                        now = ring[:, ((kt % RING) * 2 + p) * S:((kt % RING) * 2 + p + 1) * S]
                        pool.tensor_tensor(a, before, now, ALU.add).then_inc(summed, 1)

            pool.wait_ge(residual_ready, 2)
            for p in range(2):
                place_max(0, 0, p)
            for j in range(2):
                add_up(j, j, early=2 + j)
            with pool.Fori(0, ROUTE_FROM // 2 - 1) as i:
                for par in range(2):
                    add_up(2 * i + 2 + par, par)
            for b in range(B - 1):
                add_up(ROUTE_FROM + b, b % 2, routes=b)
            add_up(PAIRS - 1, 1, upto=KT - LAST_BY_PE, last=True)
            inverse_root(2 * B - 1)
            number_rows(B - 1)
            scatter(B - 1)

            pool.wait_ge(residual_stored, 16 * B)
            for e in range(E):
                for n in range(ST):
                    pool.wait_ge(ye_ready, e * ST + n + 1)
                    pool.indirect_dma_start(
                        out=out_rows, in_=ye[e % 2][:, n * D:(n + 1) * D], in_offset=None,
                        out_offset=bass.IndirectOffsetOnAxis(ap=xe(e)[:, n, W - 1:W].bitcast(U32), axis=0),
                        bounds_check=T - 1, oob_is_err=False).then_inc(stored[e % 2], 16)

        @block.scalar
        def _(act):
            def copy_turned(n, into, done, turned):
                act.wait_ge(turned, n + 1)
                act.activation(into, ps_x[n % 2][:, :], ACT.Copy).then_inc(done, 1)

            def copy_hT(b, g):
                n = 2 * b + g
                copy_turned(n, hT[:, n * HALF:(n + 1) * HALF], hT_ready, h_turned)

            for g in range(2):
                copy_hT(0, g)

            def copy_h2T(b, g):
                if b > 0:
                    act.wait_ge(logits_done, b)
                copy_turned(2 * b + g, h2T[:, g * HALF:(g + 1) * HALF], h2T_ready, h2_turned)

            def copy_sums(b, g):
                act.wait_ge(h2_ready, b + 1)
                at = b * S + g * HALF
                act.activation(rows[:, g * QT // 2:(g + 1) * QT // 2, D:2 * D],
                               x2[:, at:at + HALF].rearrange("p (t d) -> p t d", d=D), ACT.Copy).then_inc(sum_copied, 1)

            def shares(b):
                act.wait_ge(shifted, b + 1)
                e = ex[:, b * QT:(b + 1) * QT, :]
                act.activation(e, e, ACT.Exp).then_inc(route_exp, 1)

            def cast_qk(j, par, use):
                p, half = divmod(use, 2)
                c = slice(half * HALF, (half + 1) * HALF)
                b = ps_x[use % 2]
                act.wait_ge(qk_done, 4 * j + use + 1)
                act.activation(qA[par][p][0:DK, c], b[0:DK, :], ACT.Copy)
                act.activation(kA[par][p][DK:P, c], b[DK:P, :], ACT.Copy).then_inc(qk_cast, 1)

            def split_high(j, par, part):
                if part == 0:
                    act.wait_ge(qk_done, 4 * (j - 1) + 4)
                    act.wait_ge(w_loaded[par], 64 * (j // 2) + (64 if par else 48))
                if part < 2:
                    c = slice(part * HALF, (part + 1) * HALF)
                    act.activation(h_high[:, c], hTs[par][:, c], ACT.Copy).then_inc(high_split, 1)
                else:
                    act.activation(w_high[:, :], wst[par][:, 0:4 * DK], ACT.Copy).then_inc(high_split, 1)

            def cast_q_again(j, par, half):
                act.wait_ge(qk_cast, 4 * j + half + 1)
                c = slice(half * HALF, (half + 1) * HALF)
                act.activation(qA[par][0][DK:P, c], qA[par][0][0:DK, c], ACT.Copy).then_inc(q_again, 1)

            def copy_v(j, par, half):
                act.wait_ge(v_done, 2 * j + half + 1)
                act.activation(V[par][:, half * HALF:(half + 1) * HALF], ps_x[half][:, :],
                               ACT.Copy).then_inc(v_copied, 1)

            def copy_max(j, p):
                act.wait_ge(c_done, 2 * j + p + 1)
                if not (isinstance(j, int) and j == 0):
                    act.wait_ge(c_placed, 2 * j + p - 1)
                act.activation(mxr[p][DK:KB, :], ps_x[p][DK:KB, 0:P], ACT.Copy).then_inc(c_copied, 1)

            def copy_z(j, half, first=False):
                act.wait_ge(pv_done, 2 * KT * (j + 1) - 1 + half)
                if not first:
                    act.wait_ge(z_ready, 2 * j - 1 + half)
                act.activation(zr[:, half * HALF:(half + 1) * HALF], ps_z[half][:, :], ACT.Copy).then_inc(z_copied, 1)

            def unit(j, u, first):
                kt, half, p = u // 4, (u // 2) % 2, u % 2
                if not (first and kt < RING):
                    was = kt - RING if kt >= RING else kt - RING + KT
                    back = j if kt >= RING else j - 1
                    if p == 0:
                        act.wait_ge(pv_done, 2 * KT * back + 2 * was + half + 1)
                    if half == 0:
                        act.wait_ge(summed, 14 * back + 2 * (max(was, 1) - 1) + p + 1)
                act.wait_ge(scores_ready, UNITS * j + u + 1)
                act.activation(P_tile(kt, p, half), ps_s[u % 2][:, :], ACT.Exp, scale=SCALE).then_inc(exp_done, 1)

            def pair(j, par, first=False, second=False, last=False, routes=None):
                for u in range(UNITS):
                    unit(j, u, first)
                    if first or second:
                        if u in EARLY_TURN_AT[j]:
                            copy_hT(*EARLY_TURN_AT[j][u])
                    if routes is not None:
                        if u - 1 in TURN_AT:
                            copy_h2T(routes, TURN_AT[u - 1])
                        if u in SUM_COPY_AT:
                            copy_sums(routes, SUM_COPY_AT[u])
                        if u == SHARE_AT:
                            shares(routes)
                    if not last and u in QK_AT:
                        cast_qk(j + 1, 1 - par, QK_AT[u])
                    if u in SPLIT_AT and not (last or routes == B - 2):
                        split_high(j + 2, par, SPLIT_AT[u])
                    if not last and QK_AT.get(u - 1, 2) < 2:
                        cast_q_again(j + 1, 1 - par, QK_AT[u - 1])
                    if not last and u in V_AT:
                        copy_v(j + 1, 1 - par, V_AT[u])
                    if not last and u in C_AT:
                        copy_max(j + 1, C_AT[u])
                    if not first and u in Z_AT:
                        copy_z(j - 1, Z_AT[u], first=second)

            for use in range(4):
                cast_qk(0, 0, use)
                if use < 2:
                    cast_q_again(0, 0, use)
            for half in range(2):
                copy_v(0, 0, half)
            for p in range(2):
                copy_max(0, p)
            pair(0, 0, first=True)
            pair(1, 1, second=True)
            with act.Fori(0, PAIR_LOOP) as i:
                for par in range(2):
                    pair(2 * i + 2 + par, par)
            for b in range(B - 1):
                pair(ROUTE_FROM + b, b % 2, routes=b)
            pair(PAIRS - 1, (PAIRS - 1) % 2, last=True)
            for half in range(2):
                copy_z(PAIRS - 1, half)

            for g in range(2):
                copy_h2T(B - 1, g)
            for g in range(2):
                copy_sums(B - 1, g)
            shares(B - 1)

            act.wait_ge(w1_loaded, 16)
            for e in range(E):
                piece = slice(e * F, (e + 1) * F)
                act.activation(w1_high[:, piece], w1_sb[:, piece], ACT.Copy).then_inc(w1_split, 1)
            def high_tokens(e):
                act.wait_ge(xe_turned, e + 1)
                if e >= 2:
                    act.wait_ge(up_done, FC * (e - 1))
                act.activation(xeT_high[e % 2][:, :], ps_x[e % 2][:, :], ACT.Copy).then_inc(xeT_split, 1)

            high_tokens(0)
            for e in range(E):
                if e + 1 < E:
                    high_tokens(e + 1)
                if e >= 2:
                    act.wait_ge(down_done, e - 1)
                for c in range(1, FC, 2):
                    act.wait_ge(up_done, e * FC + c + 1)
                    act.activation(rT[e % 2][:, c * HALF:(c + 1) * HALF], ps_s[1][:, :],
                                   ACT.Relu).then_inc(relu_done[1], 1)

        @block.vector
        def _(dve):
            dve.memset(ident[:, :], 1.0).then_inc(dve_consts, 1)
            dve.memset(rowmask[:, :], 1.0).then_inc(dve_consts, 1)
            dve.memset(upper[:, :], 1.0).then_inc(dve_consts, 1)
            dve.memset(hot_b[:, :, QT * E:(QT + 1) * E], 0.0).then_inc(dve_consts, 1)
            dve.memset(seen[:, 0, :], 0.0).then_inc(dve_consts, 1)
            dve.memset(ones[:, :], 1.0).then_inc(dve_consts, 1)
            dve.memset(ones_b[:, :], 1.0).then_inc(dve_consts, 1)
            for p in range(2):
                dve.memset(mxw[p][:, :], 0.0).then_inc(dve_consts, 1)
            steps = [0]

            def then(ins):
                steps[0] += 1
                ins.then_inc(chain, 1)
                dve.wait_ge(chain, steps[0])

            def find_moments(n, b):
                if n > 0:
                    dve.wait_ge(moments_ready, n)
                for t in range(QT):
                    i = b * QT + t
                    ins = dve.bn_stats(moment_parts[:, t, :], x2[:, i * D:(i + 1) * D])
                then(ins)
                for t in range(QT):
                    ins = dve.bn_aggr(moments[:, n, t, :], moment_parts[:, t, :])
                ins.then_inc(moments_ready, 1)

            def normalise(n, b, tile, done):
                dve.wait_ge(moments_ready, n + 1)
                dve.wait_ge(root_ready, n + 1)
                for t in range(QT):
                    i = b * QT + t
                    ins = dve.tensor_scalar(tile(t), x2[:, i * D:(i + 1) * D], moments[:, n, t, 0:1],
                                            roots[:, n, 1, t:t + 1], ALU.subtract, ALU.mult)
                ins.then_inc(done, 1)

            def first_moments(b):
                dve.wait_ge(x_loaded[b], 16)
                find_moments(b, b)

            def first_norm(b):
                if b >= 2:
                    dve.wait_ge(residual_ready, b - 1)
                    dve.wait_ge(h_turned, 2 * (b - 1))
                normalise(b, b, lambda t: h_tok(b)[:, t, :], h_ready)

            def clear_rows():
                dve.wait_ge(residual_ready, B)
                dve.wait_ge(h_turned, 2 * B)
                dve.memset(rows[:, :, :], 0.0).then_inc(rows_cleared, 1)
                dve.wait_ge(rows_cleared, 1)
                dve.memset(rows[:, :, W - 1].bitcast(I32), T).then_inc(rows_cleared, 1)

            first_moments(0)
            first_moments(1)
            first_norm(0)
            for i in range(2):
                for p in range(2):
                    dve.memset(kB[i][p][DK:KB, :].bitcast(F32), -1.0).then_inc(dve_consts, 1)
            first_norm(1)

            def wide(a):
                return a.rearrange("p (t o) -> p t o", o=1).to_broadcast([P, QT, E])

            def of(b):
                t = slice(b * QT, (b + 1) * QT)
                return [a[:, t, :] for a in (lg, ex, hot)] + [cols[:, k, t] for k in range(6)]

            def second_moments(b):
                dve.wait_ge(wo_added, 2 * HP * (b + 1))
                find_moments(B + b, b)

            def second_norm(b):
                dve.wait_ge(row_numbers, b + 1)
                normalise(B + b, b, lambda t: rows[:, t, 0:D], h2_ready)

            def choose(b):
                l, x, h, top, total, first_e, rank, past, slot = of(b)
                dve.wait_ge(logits_done, b + 1)
                dve.wait_ge(consts, 4)
                then(dve.tensor_copy(l, ps_x[0][:, 0:QT * E].rearrange("p (t e) -> p t e", e=E)))
                then(dve.tensor_reduce(top, l, AX_X, ALU.max))
                dve.tensor_tensor(x, l, wide(top), ALU.subtract).then_inc(shifted, 1)
                then(dve.tensor_tensor(h, l, wide(top), ALU.is_equal))
                then(dve.scalar_tensor_tensor(out=l, in0=h, scalar=-float(E), in1=iota_e, op0=ALU.mult, op1=ALU.add))
                then(dve.tensor_reduce(first_e, l, AX_X, ALU.min))
                then(dve.tensor_tensor(h, l, wide(first_e), ALU.is_equal))
                dve.tensor_copy(hot_b[:, b, 0:QT * E].rearrange("p (t e) -> p t e", e=E), h).then_inc(onehot_ready, 1)

            def find_slots(b):
                l, x, h, top, total, first_e, rank, past, slot = of(b)
                base = seen[:, b, :].rearrange("p (o e) -> p o e", o=1)
                made = ps_x[1][:, 0:(QT + 1) * E].rearrange("p (t e) -> p t e", e=E)
                dve.wait_ge(ranks_done, b + 1)
                then(dve.tensor_tensor(l, made[:, 0:QT, :], base.to_broadcast([P, QT, E]), ALU.add))
                dve.tensor_tensor(seen[:, b + 1:b + 2, :], made[:, QT:QT + 1, :], base, ALU.add)
                then(dve.tensor_tensor(l, h, l, ALU.mult))
                then(dve.tensor_reduce(rank, l, AX_X, ALU.add))
                dve.tensor_scalar(past, rank, float(CAP), float(E * CAP), ALU.is_ge, ALU.mult)
                then(dve.tensor_scalar(slot, first_e, float(E), float(CAP), ALU.add, ALU.mult))
                then(dve.tensor_tensor(slot, slot, rank, ALU.add))
                dve.tensor_tensor(scatter_at[:, b * QT:(b + 1) * QT], slot, past, ALU.add)
                dve.wait_ge(route_exp, b + 1)
                then(dve.tensor_reduce(total, x, AX_X, ALU.add))
                dve.reciprocal(rows[:, :, 2 * D], total).then_inc(index_ready, 1)

            def low_qk(j, par, use, of_q):
                p, half = divmod(use, 2)
                c = slice(half * HALF, (half + 1) * HALF)
                b = ps_x[use % 2]
                if of_q:
                    dve.wait_ge(qk_cast, 4 * j + use + 1)
                    dve.tensor_tensor(qB[par][p][0:DK, c], b[0:DK, :], qA[par][p][0:DK, c].bitcast(F32), ALU.subtract)
                else:
                    dve.tensor_tensor(kA[par][p][0:DK, c], b[DK:P, :], kA[par][p][DK:P, c].bitcast(F32),
                                      ALU.subtract).then_inc(qk_low, 1)

            def reduce_max(j, m):
                p, qt, kh = m // 16, (m // 2) % 8, m % 2
                dve.wait_ge(m_done, UNITS * j + m + 1)
                dve.tensor_reduce(mxp[p][:, qt, kh:kh + 1], ps_m[m % 2][:, :], AX_X, ALU.max).then_inc(maxed, 1)
                if m % 16 == 15:
                    dve.wait_ge(maxed, UNITS * j + m + 1)
                    dve.tensor_reduce(mxw[p][:, DK:KB], mxp[p][:, :, :], AX_X, ALU.max).then_inc(mx_ready, 1)

            def recip(j, half, quarter):
                c = half * HALF + quarter * P
                if quarter == 0:
                    dve.wait_ge(sums_done, 2 * j + half + 1)
                dve.reciprocal(rc[:, c:c + P], ps_x[half][:, quarter * P:(quarter + 1) * P]).then_inc(recip_done, 1)
                if quarter == 3:
                    dve.wait_ge(recip_done, 8 * j + 4 * half + 4)
                    dve.wait_ge(z_copied, 2 * j + half + 1)
                    d = slice(half * HALF, (half + 1) * HALF)
                    dve.tensor_tensor(zT[:, d], zr[:, d], rc[:, d], ALU.mult).then_inc(z_ready, 1)

            def add_wo(j, g):
                dve.wait_ge(wo_done, 2 * j + g + 1)
                at = x2[:, bass.ds((j // HP) * S + g * HALF, HALF)]
                dve.tensor_tensor(at, ps_x[g][:, :], at, ALU.add).then_inc(wo_added, 1)

            def pair(j, par, first=False, second=False, last=False, routes=None):
                for u in range(UNITS + 1):
                    if first or second:
                        if u == STATS_AT:
                            first_moments(2 + j)
                        if u == NORM_AT:
                            first_norm(2 + j)
                    if second and u == UNITS:
                        clear_rows()
                    if routes is not None:
                        if u == STATS_AT:
                            second_moments(routes)
                        if u == NORM_AT:
                            second_norm(routes)
                        if u - 1 == LOGITS_AT:
                            choose(routes)
                        if u - 1 == RANKS_AT:
                            find_slots(routes)
                    if not last:
                        for m in max_units(u):
                            reduce_max(j + 1, m)
                        if u - LOW_Q in QK_AT:
                            low_qk(j + 1, 1 - par, QK_AT[u - LOW_Q], True)
                        if u - LOW_K in QK_AT:
                            low_qk(j + 1, 1 - par, QK_AT[u - LOW_K], False)
                    if not (first or second) and u - 1 in WO_AT:
                        add_wo(j - 2, WO_AT[u - 1])
                    if not first and u in RECIP_AT:
                        recip(j - 1, *RECIP_AT[u])

            for use in range(4):
                low_qk(0, 0, use, True)
                low_qk(0, 0, use, False)
            for m in range(UNITS):
                reduce_max(0, m)
            pair(0, 0, first=True)
            pair(1, 1, second=True)
            with dve.Fori(0, PAIR_LOOP) as i:
                for par in range(2):
                    pair(2 * i + 2 + par, par)
            for b in range(B - 1):
                pair(ROUTE_FROM + b, b % 2, routes=b)
            pair(PAIRS - 1, 1, last=True)
            for g in range(2):
                add_wo(PAIRS - 2, g)
            for n in range(8):
                recip(PAIRS - 1, *divmod(n, 4))
            for g in range(2):
                add_wo(PAIRS - 1, g)

            second_moments(B - 1)
            second_norm(B - 1)
            choose(B - 1)
            find_slots(B - 1)

            def finish(e):
                dve.wait_ge(down_done, e + 1)
                if e >= 2:
                    dve.wait_ge(stored[e % 2], 16 * ST * (e // 2))
                for n in range(ST):
                    dve.scalar_tensor_tensor(out=ye[e % 2][:, n * D:(n + 1) * D], in0=ps_z[e % 2][:, n * D:(n + 1) * D],
                                             scalar=xe(e)[:, n, 2 * D:2 * D + 1], in1=xe(e)[:, n, D:2 * D],
                                             op0=ALU.mult, op1=ALU.add).then_inc(ye_ready, 1)

            def low_tokens(e):
                dve.wait_ge(xeT_split, e + 1)
                dve.tensor_tensor(xeT_low[e % 2][:, :], ps_x[e % 2][:, :], xeT_high[e % 2][:, :].bitcast(F32),
                                  ALU.subtract).then_inc(xeT_ready, 1)

            for e in range(E):
                piece = slice(e * F, (e + 1) * F)
                dve.wait_ge(w1_split, e + 1)
                dve.tensor_tensor(w1_low[:, piece], w1_sb[:, piece], w1_high[:, piece].bitcast(F32),
                                  ALU.subtract).then_inc(w1_ready, 1)
            low_tokens(0)
            for e in range(E):
                if e >= 2:
                    dve.wait_ge(down_done, e - 1)
                for c in range(0, FC, 2):
                    dve.wait_ge(up_done, e * FC + c + 1)
                    dve.tensor_scalar(rT[e % 2][:, c * HALF:(c + 1) * HALF], ps_s[0][:, :], 0.0, None,
                                      ALU.max).then_inc(relu_done[0], 1)
                    if c == 0 and e >= 2:
                        finish(e - 2)
                if e + 1 < E:
                    low_tokens(e + 1)
            finish(E - 2)
            finish(E - 1)

        @block.tensor
        def _(pe):
            pe.wait_ge(consts, 4)
            pe.wait_ge(dve_consts, 9)
            def turn_h(b, g):
                pe.wait_ge(h_ready, b + 1)
                for i in range(4):
                    mm = pe.transpose(ps_x[g][:, i * P:(i + 1) * P], h_tok(b)[:, 4 * g + i, :], ident[:, :])
                mm.then_inc(h_turned, 1)

            def turned(j, par):
                return hT if isinstance(j, int) and j == 0 else hTs[par]

            def project_qk(j, par, use):
                p, half = divmod(use, 2)
                w, c = slice(p * P, (p + 1) * P), slice(half * HALF, (half + 1) * HALF)
                bank = ps_x[use % 2][:, :]
                if isinstance(j, int) and j < 2:
                    pe.wait_ge(w_loaded[par], 64 if par else 48)
                    mm = pe.matmul(bank, wst[par][:, w], turned(j, par)[:, c], start=True, stop=True)
                else:
                    pe.wait_ge(low_split, 2 * (j - 2) + 2)
                    pe.matmul(bank, w_low[:, w], h_high[:, c], start=True, stop=False)
                    pe.matmul(bank, w_high[:, w], h_low[:, c], start=False, stop=False)
                    mm = pe.matmul(bank, w_high[:, w], h_high[:, c], start=False, stop=True)
                mm.then_inc(qk_done, 1)

            def project_v(j, par, half):
                pe.wait_ge(qk_low, 4 * j + 2 + half + 1)
                pe.wait_ge(w_loaded[par], 64 * (j // 2) + (64 if par else 48))
                for i in range(4):
                    t = 4 * half + i
                    mm = pe.matmul(ps_x[half][:, i * P:(i + 1) * P], turned(j, par)[:, t * P:(t + 1) * P],
                                   wst[par][:, 4 * DK:6 * DK], start=True, stop=True)
                mm.then_inc(v_done, 1)

            def max_scores(j, par, m):
                p, qt, kh = m // 16, (m // 2) % 8, m % 2
                if m % 16 == 0:
                    pe.wait_ge(qk_low, 4 * j + 2 * p + 2)
                    if p == 0:
                        pe.wait_ge(q_again, 2 * j + 2)
                    else:
                        pe.wait_ge(qk_copied, 64 * j + 64)
                if not (isinstance(j, int) and j == 0 and m < 2):
                    pe.wait_ge(maxed, UNITS * j + m - 1)
                pe.matmul(ps_m[m % 2][:, :], qA[par][p][:, qt * P:(qt + 1) * P],
                          kA[par][p][:, kh * HALF:(kh + 1) * HALF], start=True, stop=True).then_inc(m_done, 1)

            def turn_max(j, p):
                pe.wait_ge(mx_ready, 2 * j + p + 1)
                pe.transpose(ps_x[p][0:KB, 0:P], mxw[p][:, :], ident[:, :]).then_inc(c_done, 1)

            def scores(j, par, u):
                kt, half, p = u // 4, (u // 2) % 2, u % 2
                if isinstance(j, int) and j == 0 and u == 0:
                    pe.wait_ge(dve_consts, 13)
                if u == 0:
                    pe.wait_ge(k_copied, 32 * j + 32)
                if u < 2:
                    pe.wait_ge(c_placed, 2 * j + u + 1)
                if not (isinstance(j, int) and j == 0 and u < 2):
                    pe.wait_ge(exp_done, UNITS * j + u - 1)
                c = slice(half * HALF, (half + 1) * HALF)
                k = slice(kt * P, (kt + 1) * P)
                pe.matmul(ps_s[u % 2][:, :], kA[par][p][:, k], qA[par][p][:, c], start=True, stop=False)
                pe.matmul(ps_s[u % 2][:, :], kB[par][p][:, k], qB[par][p][:, c], start=False,
                          stop=True).then_inc(scores_ready, 1)

            def values(j, par, kt, half, first=False):
                if kt == 0:
                    pe.wait_ge(v_copied, 2 * j + 2)
                    if not first:
                        pe.wait_ge(z_copied, 2 * j - 1 + half)
                for p in range(2):
                    mm = pe.matmul(ps_z[half][p * DK:(p + 1) * DK, :],
                                   V[par][:, kt * P + p * DK:kt * P + (p + 1) * DK], P_tile(kt, p, half),
                                   start=(kt == 0), stop=(kt == KT - 1))
                mm.then_inc(pv_done, 1)

            def softmax_sums(j, par, half, by_pe=0):
                pe.wait_ge(summed, 14 * j + 14 - 2 * by_pe)
                for p in range(2):
                    at = p * S + half * HALF
                    parts = [acc[par][:, at:at + HALF]] + [P_tile(kt, p, half) for kt in range(KT - by_pe, KT)]
                    for i, part in enumerate(parts):
                        mm = pe.matmul(ps_x[half][p * DK:(p + 1) * DK, :], ones[:, :], part,
                                       start=(i == 0), stop=(i == len(parts) - 1))
                mm.then_inc(sums_done, 1)

            def project_out(j, par, g):
                pe.wait_ge(wo_loaded[par], 16 * (j // 2) + 16)
                pe.wait_ge(z_ready, 2 * j + g + 1)
                for i in range(4):
                    t = 4 * g + i
                    mm = pe.matmul(ps_x[g][:, i * P:(i + 1) * P], zT[:, t * P:(t + 1) * P], wo[par][:, :],
                                   start=True, stop=True)
                mm.then_inc(wo_done, 1)

            def turn_h2(b, g):
                pe.wait_ge(h2_ready, b + 1)
                for i in range(4):
                    mm = pe.transpose(ps_x[g][:, i * P:(i + 1) * P], rows[:, 4 * g + i, 0:D], ident[:, :])
                mm.then_inc(h2_turned, 1)

            def make_logits(b):
                pe.wait_ge(wr_loaded, 16)
                pe.wait_ge(h2T_ready, 2 * b + 2)
                for t in range(QT):
                    mm = pe.matmul(ps_x[0][:, t * E:(t + 1) * E], h2T[:, t * P:(t + 1) * P], wr[:, :],
                                   start=True, stop=True)
                mm.then_inc(logits_done, 1)

            def count_ranks(b):
                pe.wait_ge(onehot_ready, b + 1)
                made = ps_x[1][:, 0:(QT + 1) * E].rearrange("p (t e) -> p t e", e=E)
                pe.matmul(ps_x[1][:, 0:(QT + 1) * E], upper[:, :], hot_b[:, b, :], start=True, stop=False,
                          skip_group_check=True)
                for t in range(QT):
                    one = hot_b[:, b, t * E:(t + 1) * E].rearrange("p (o e) -> p o e", o=1)
                    mm = pe.matmul(made[:, t + 1:QT + 1, :], ones_b[:, :], one.to_broadcast([P, QT - t, E]),
                                   start=False, stop=(t == QT - 1), skip_group_check=True)
                mm.then_inc(ranks_done, 1)

            def pair(j, par, first=False, second=False, last=False, routes=None):
                nxt = 1 - par
                for u in range(UNITS):
                    kt, odd = u // 4, u % 4
                    scores(j, par, u)
                    ms = list(max_units(u)) if not last else []
                    for m in ms[:1]:
                        max_scores(j + 1, nxt, m)
                    if odd in (1, 3) and (kt > 0 or not first):
                        half = odd // 2
                        if kt > 0:
                            values(j, par, kt - 1, half, first)
                        else:
                            values(j - 1, nxt, KT - 1, half, second)
                    if not last and u in QK_AT:
                        use = QK_AT[u]
                        if use >= 2:
                            pe.wait_ge(qk_low, 4 * (j + 1) + use - 1)
                        elif first or second:
                            pe.wait_ge(c_copied, 2 * j + use + 1)
                        else:
                            pe.wait_ge(recip_done, 8 * (j - 2) + 4 * use + 4)
                        project_qk(j + 1, nxt, use)
                    if not last and u in V_AT:
                        project_v(j + 1, nxt, V_AT[u])
                    if (first or second) and u in EARLY_TURN_AT[j]:
                        b, g = EARLY_TURN_AT[j][u]
                        if u < min(C_AT):
                            pe.wait_ge(v_copied, 2 * (j + 1) + g + 1)
                        elif g == 0:
                            pe.wait_ge(c_copied, 2 * (j + 1) + 1)
                        else:
                            pe.wait_ge(hT_ready, 2 * b)
                        turn_h(b, g)
                    if routes is not None and u in TURN_AT:
                        pe.wait_ge(v_copied, 2 * (j + 1) + TURN_AT[u] + 1)
                        turn_h2(routes, TURN_AT[u])
                    if not (first or second) and u in WO_AT:
                        if last:
                            pe.wait_ge(recip_done, 8 * (j - 2) + 4 * WO_AT[u] + 4)
                        elif routes is not None:
                            pe.wait_ge(h2T_ready, 2 * routes + WO_AT[u] + 1)
                        else:
                            pe.wait_ge(v_copied, 2 * (j + 1) + WO_AT[u] + 1)
                        project_out(j - 2, par, WO_AT[u])
                    if not last and u in C_AT:
                        p = C_AT[u]
                        if first or second:
                            pe.wait_ge(hT_ready, max(2 * b + g + 1 for v, (b, g) in EARLY_TURN_AT[j].items()
                                                     if v < u and g == p))
                        elif routes is not None and p == 1:
                            pe.wait_ge(index_ready, routes + 1)
                        else:
                            pe.wait_ge(wo_added, 2 * (j - 2) + p + 1)
                        turn_max(j + 1, p)
                    if routes is not None and u == LOGITS_AT:
                        pe.wait_ge(c_copied, 2 * (j + 1) + 1)
                        make_logits(routes)
                    if routes is not None and u == RANKS_AT:
                        pe.wait_ge(wo_added, 2 * (j - 2) + 2)
                        count_ranks(routes)
                    if not first and u in SUM_AT:
                        half = SUM_AT[u]
                        if last:
                            pe.wait_ge(wo_added, 2 * (j - 2) + half + 1)
                        elif routes is not None and half == 0:
                            pe.wait_ge(onehot_ready, routes + 1)
                        else:
                            pe.wait_ge(c_copied, 2 * (j + 1) + half + 1)
                        softmax_sums(j - 1, nxt, half)
                    for m in ms[1:]:
                        max_scores(j + 1, nxt, m)

            for g in range(2):
                turn_h(0, g)
            for use in range(4):
                if use < 2:
                    pe.wait_ge(hT_ready, 2)
                else:
                    pe.wait_ge(qk_low, use - 1)
                project_qk(0, 0, use)
            for half in range(2):
                project_v(0, 0, half)
            for m in range(UNITS):
                max_scores(0, 0, m)
                if m in (UNITS // 2 + 2, UNITS - 1):
                    p = m // (UNITS - 1)
                    pe.wait_ge(v_copied, p + 1)
                    turn_max(0, p)
            pair(0, 0, first=True)
            pair(1, 1, second=True)
            with pe.Fori(0, PAIR_LOOP) as i:
                for par in range(2):
                    pair(2 * i + 2 + par, par)
            for b in range(B - 1):
                pair(ROUTE_FROM + b, b % 2, routes=b)
            last = PAIRS - 1
            pair(last, 1, last=True)
            pe.wait_ge(exp_done, UNITS * PAIRS)
            for half in range(2):
                values(last, 1, KT - 1, half)
            for g in range(2):
                pe.wait_ge(recip_done, 8 * (last - 1) + 4 * g + 4)
                project_out(last - 1, 0, g)
            for half in range(2):
                pe.wait_ge(wo_added, 2 * (last - 1) + half + 1)
                softmax_sums(last, 1, half, LAST_BY_PE)
            for g in range(2):
                project_out(last, 1, g)

            pe.wait_ge(wo_added, 2 * PAIRS)
            for g in range(2):
                turn_h2(B - 1, g)
            make_logits(B - 1)
            count_ranks(B - 1)

            def turn_tokens(e):
                pe.wait_ge(xe_loaded[e % XE], 16 * (e // XE + 1))
                if e >= 2:
                    pe.wait_ge(xeT_ready, e - 1)
                for i in range(ST):
                    mm = pe.transpose(ps_x[e % 2][:, i * P:(i + 1) * P], xe(e)[:, i, 0:D], ident[:, :])
                mm.then_inc(xe_turned, 1)

            def down(e):
                if e >= 2:
                    pe.wait_ge(ye_ready, ST * (e - 1))
                for i in range(2):
                    pe.wait_ge(relu_done[i], FC // 2 * (e + 1))
                for st in range(ST):
                    for c in range(FC):
                        mm = pe.matmul(ps_z[e % 2][:, st * P:(st + 1) * P],
                                       rT[e % 2][:, c * HALF + st * P:c * HALF + (st + 1) * P],
                                       w2_sb[:, (c * E + e) * D:(c * E + e + 1) * D], start=(c == 0), stop=(c == FC - 1))
                mm.then_inc(down_done, 1)

            pe.wait_ge(w1_ready, E)
            pe.wait_ge(w2_loaded, 16 * FC)
            turn_tokens(0)
            for e in range(E):
                if e + 1 < E:
                    turn_tokens(e + 1)
                pe.wait_ge(xeT_ready, e + 1)
                for c in range(FC):
                    n = e * FC + c
                    if n >= 2:
                        pe.wait_ge(relu_done[n % 2], n // 2)
                    w = slice(e * F + c * P, e * F + (c + 1) * P)
                    pe.matmul(ps_s[n % 2][:, :], w1_low[:, w], xeT_high[e % 2][:, :], start=True, stop=False)
                    pe.matmul(ps_s[n % 2][:, :], w1_high[:, w], xeT_low[e % 2][:, :], start=False, stop=False)
                    pe.matmul(ps_s[n % 2][:, :], w1_high[:, w], xeT_high[e % 2][:, :], start=False,
                              stop=True).then_inc(up_done, 1)
                if e >= 1:
                    down(e - 1)
            down(E - 1)


_INS = ["L0_attn_x", "L0_attn_w_q", "L0_attn_w_k", "L0_attn_w_v", "L0_attn_w_o", "L0_ffn_Wr", "L0_ffn_W1", "L0_ffn_W2"]


def kernel(**inputs):
    import numpy as _np
    import concourse.bacc as _bacc
    from concourse import mybir as _mybir
    from concourse.bass_utils import run_bass_kernel_spmd as _run

    nc = _bacc.Bacc("TRN2", target_bir_lowering=False, num_devices=1)
    arrays, args = {}, []
    for name in _INS:
        a = _np.ascontiguousarray(inputs[name])
        arrays[f"in_{name}"] = a
        args.append(nc.dram_tensor(f"in_{name}", a.shape, _mybir.dt.from_np(a.dtype), kind="ExternalInput").ap())
    shape = inputs["L0_attn_x"].shape
    args.append(nc.dram_tensor("out_0", shape, _mybir.dt.float32, kind="ExternalOutput").ap())
    block_kernel(nc, *args)
    r = _run(nc, [arrays], core_ids=[0])
    return r.results[0]["out_0"]
```
